# Optimizing a Trainium2 kernel written in Bass

```python
import numpy as np
import jax
import jax.numpy as jnp

def _softmax(x, axis=-1):
    return jax.nn.softmax(x, axis=axis)

def _gelu(x):
    return jax.nn.gelu(x, approximate=True)

def _silu(x):
    return jax.nn.silu(x)

def _sigmoid(x):
    return jax.nn.sigmoid(x)

def _layernorm(x, axis=-1, eps=1e-05):
    m = jnp.mean(x, axis=axis, keepdims=True)
    v = jnp.var(x, axis=axis, keepdims=True)
    return (x - m) / jnp.sqrt(v + eps)

def _scatter_add(tgt, idx, src, axis=0):
    return tgt.at[idx].add(src)

def _segment_sum(src, seg, n):
    return jax.ops.segment_sum(src, seg, n)
kernel_name = 'mk_adj_ffn_d1_adj_r2_bff4db'

def setup_inputs(seed: int=0):
    np.random.seed(seed)
    _w = jnp.asarray

    def _rec_inputs():
        import jax
        import jax.numpy as jnp
        _gk = jax.random.key(seed)
        x = -0.0002928 + 1 * jax.random.normal(jax.random.fold_in(_gk, 1), (64, 128, 128), jnp.float32)
        _w = (1.0 + jnp.arange(128, dtype=jnp.float32)) ** (-0.5)
        _w = _w / _w.mean()
        _pij = jnp.clip(0.03125 * _w[:, None] * _w[None, :], 0.0, 1.0)
        _a = jax.random.uniform(jax.random.fold_in(_gk, 2), (64, 128, 128)) < _pij
        adj = _a.astype(jnp.int32)
        return (x, adj)
    x, adj = _rec_inputs()

    def _L0_gnn_setup():
        import jax, jax.numpy as jnp
        import numpy as np
        ALPHA = 0.2
        NEG_BIG = -9000000000000000.0
        key = jax.random.key(seed)
        k1, k2, k3, k4 = jax.random.split(key, 4)
        B, N, Fin, Fout = (8, 1024, 128, 128)
        h = jax.random.normal(k1, (B, N, Fin), dtype=jnp.float32)
        adj = jax.random.randint(k2, (B, N, N), 0, 2, dtype=jnp.int32)
        gain = 1.414
        limW = gain * np.sqrt(6.0 / (Fin + Fout))
        W = jax.random.uniform(k3, (Fin, Fout), dtype=jnp.float32, minval=-limW, maxval=limW)
        lima = gain * np.sqrt(6.0 / (2 * Fout + 1))
        a = jax.random.uniform(k4, (2 * Fout, 1), dtype=jnp.float32, minval=-lima, maxval=lima)
        return {'h': h, 'adj': adj, 'W': W, 'a': a}
    _L0_gnn_all = _L0_gnn_setup()
    _L0_gnn_in = {k: v for k, v in _L0_gnn_all.items() if k in ('W', 'a')}
    del _L0_gnn_all

    def _L0_ffn_setup():
        import jax, jax.numpy as jnp
        import numpy as np
        D_MODEL = 128
        N_EXPERTS = 16
        HIDDEN = 256
        SCALE = 0.02
        key = jax.random.key(seed)
        ks = jax.random.split(key, 5)
        x = jax.random.normal(ks[0], (4, 4096, D_MODEL), dtype=jnp.float32)
        gate_w = jax.random.normal(ks[1], (D_MODEL, N_EXPERTS), dtype=jnp.float32) * SCALE
        gate_b = jnp.zeros((N_EXPERTS,), dtype=jnp.float32)
        w1 = jax.random.normal(ks[2], (N_EXPERTS, D_MODEL, HIDDEN), dtype=jnp.float32) * SCALE
        w2 = jax.random.normal(ks[3], (N_EXPERTS, D_MODEL, HIDDEN), dtype=jnp.float32) * SCALE
        w3 = jax.random.normal(ks[4], (N_EXPERTS, HIDDEN, D_MODEL), dtype=jnp.float32) * SCALE
        return {'x': x, 'gate_w': gate_w, 'gate_b': gate_b, 'w1': w1, 'w2': w2, 'w3': w3}
    _L0_ffn_all = _L0_ffn_setup()
    _L0_ffn_in = {k: v for k, v in _L0_ffn_all.items() if k in ('gate_w', 'gate_b', 'w1', 'w2', 'w3')}
    del _L0_ffn_all
    return {'x': x, 'adj': adj, 'L0_gnn_W': _L0_gnn_in['W'], 'L0_gnn_a': _L0_gnn_in['a'], 'L0_ffn_gate_w': _L0_ffn_in['gate_w'], 'L0_ffn_gate_b': _L0_ffn_in['gate_b'], 'L0_ffn_w1': _L0_ffn_in['w1'], 'L0_ffn_w2': _L0_ffn_in['w2'], 'L0_ffn_w3': _L0_ffn_in['w3']}

def reference(x, adj, L0_gnn_W, L0_gnn_a, L0_ffn_gate_w, L0_ffn_gate_b, L0_ffn_w1, L0_ffn_w2, L0_ffn_w3):
    import jax
    import jax.numpy as jnp

    def _L0_gnn_ref(h, adj, W, a):
        import jax, jax.numpy as jnp
        import numpy as np
        ALPHA = 0.2
        NEG_BIG = -9000000000000000.0
        Wh = jnp.matmul(h, W)
        Fout = W.shape[1]
        a1 = a[:Fout, 0]
        a2 = a[Fout:, 0]
        s1 = jnp.einsum('bnf,f->bn', Wh, a1)
        s2 = jnp.einsum('bnf,f->bn', Wh, a2)
        e = jax.nn.leaky_relu(s1[:, :, None] + s2[:, None, :], negative_slope=ALPHA)
        masked = jnp.where(adj > 0, e, jnp.full_like(e, NEG_BIG))
        attention = jax.nn.softmax(masked, axis=2)
        h_prime = jnp.matmul(attention, Wh)
        return jax.nn.elu(h_prime)

    def _L0_ffn_ref(x, gate_w, gate_b, w1, w2, w3):
        import jax, jax.numpy as jnp
        import numpy as np
        D_MODEL = 128
        N_EXPERTS = 16
        HIDDEN = 256
        SCALE = 0.02
        n_experts = w1.shape[0]
        logits = jnp.einsum('bsd,de->bse', x, gate_w) + gate_b
        probs = jax.nn.softmax(logits, axis=-1)
        top_probs, top_idx = jax.lax.top_k(probs, 2)
        top_probs = top_probs / jnp.sum(top_probs, axis=-1, keepdims=True)
        dispatch = jnp.sum(jax.nn.one_hot(top_idx, n_experts, dtype=x.dtype) * top_probs[..., None], axis=-2)
        h1 = jnp.einsum('bsd,edh->bseh', x, w1)
        h2 = jnp.einsum('bsd,edh->bseh', x, w2)
        hidden = jax.nn.silu(h1) * h2
        expert_out = jnp.einsum('bseh,eho->bseo', hidden, w3)
        return jnp.einsum('bseo,bse->bso', expert_out, dispatch)
    x = x + _L0_gnn_ref(_layernorm(x, axis=-1), adj, L0_gnn_W, L0_gnn_a)
    x = x + _L0_ffn_ref(_layernorm(x, axis=-1), L0_ffn_gate_w, L0_ffn_gate_b, L0_ffn_w1, L0_ffn_w2, L0_ffn_w3)
    return x

_drawn_inputs = setup_inputs


def setup_inputs(seed=0):
    import zlib

    import numpy as np

    out = dict(_drawn_inputs(seed))
    spreads = {'L0_ffn_gate_b': (0.0, 0.8)}
    factors = {'L0_ffn_gate_w': 8.0, 'L0_ffn_w1': 8.0, 'L0_ffn_w2': 8.0, 'L0_ffn_w3': 8.0}
    for name, (base, spread) in spreads.items():
        noise = np.random.default_rng([zlib.crc32(name.encode()), seed]).standard_normal(out[name].shape)
        drawn = base * np.exp(spread * noise) if base else spread * noise
        out[name] = jnp.asarray(drawn.astype(out[name].dtype))
    for name, factor in factors.items():
        out[name] = (out[name] * factor).astype(out[name].dtype)
    return out
```

```python
from contextlib import ExitStack

import concourse.bass as bass
from concourse import mybir

F32 = mybir.dt.float32
F16 = mybir.dt.float16
BF16 = mybir.dt.bfloat16
I32 = mybir.dt.int32
U32 = mybir.dt.uint32
ALU = mybir.AluOpType
ACT = mybir.ActivationFunctionType
AX_X = mybir.AxisListType.X

P = 128
EPS = 1e-5
ALPHA = 0.2
NEG_BIG = -9000000000000000.0


def gnn_moe_kernel(nc, x, adj, gnn_w, gnn_a, gate_w, gate_b, w1, w2, w3, out):
    B, N, D = x.shape
    E, _, H = w1.shape
    assert N == P and D == P and H == 2 * P and E == 16
    Q = 4
    GROUPS = B // Q
    TOKENS = B * N
    K = 2
    REGION = TOKENS + P
    assert REGION % P == 0
    NOWHERE = K * TOKENS
    ROW = D + 4
    U = 8
    TILES = -(-(K * TOKENS // P + E - 1) // U) * U
    COUNT_BASE = REGION // P

    rows_dram = nc.dram_tensor("dispatched_rows", [E * REGION + P, ROW], F32).ap()
    result_dram = nc.dram_tensor("expert_results", [K * TOKENS, D], F32).ap()

    ctx = ExitStack()
    with ctx:
        def sb(name, shape, dt):
            return ctx.enter_context(nc.sbuf_tensor(name, shape, dt))

        def sem(name):
            return ctx.enter_context(nc.semaphore(name))

        bank = [ctx.enter_context(nc.psum_tensor(f"bank{i}", [P, 512], F32)) for i in range(8)]
        hT_ps, z_ps, wh_ps, pT_ps, o_ps, h2T_ps, logit_ps, rank_ps = bank
        xT_ps, mlp_ps, gT_ps, y_ps = bank[0:2], bank[2:4], bank[4:6], bank[6:8]

        x_all = sb("x_all", [P, B * D], F32)
        w12 = sb("w12", [P, E * 2 * H], F32)
        w3s = sb("w3s", [P, E * 2 * D], F32)
        ident = sb("ident", [P, P], F32)
        ident_b = sb("ident_b", [P, P], BF16)
        before = sb("before", [P, P], F16)
        ones_h = sb("ones_h", [P, P], F16)
        ones_row = sb("ones_row", [1, P], F32)
        expert_no = sb("expert_no", [P, E], F32)
        dest_all = sb("dest_all", [P, K, B], I32)
        eps_col = sb("eps_col", [P, 1], F32)
        zero_rows = sb("zero_rows", [P, ROW], F32)
        tile_no = sb("tile_no", [P, U], F32)
        region_no = sb("region_no", [P, E], F32)
        gw = sb("gw", [P, D], F32)
        gwT = sb("gwT", [P, D], F32)
        a_col = sb("a_col", [P, 2], F32)
        a_rep = sb("a_rep", [P, 2, P], F32)
        wa_rep = sb("wa_rep", [P, 2, P], F32)
        gate_ws = sb("gate_ws", [P, E], F32)
        bias_row = sb("bias_row", [1, Q, E], F32)
        adj_s = sb("adj_s", [P, 2, Q * N], I32)
        mask = sb("mask", [P, 2, Q * N], BF16)
        x_stats = sb("x_stats", [P, Q, 6], F32)
        x2_stats = sb("x2_stats", [P, Q, 6], F32)
        mv = sb("mv", [P, 2 * Q, 2], F32)
        lnv = sb("lnv", [P, 2 * Q], F32)
        rs0 = sb("rs0", [P, 2 * Q], F32)
        rs1 = sb("rs1", [P, 2 * Q], F32)
        rs2 = sb("rs2", [P, 2 * Q], F32)
        rstd = sb("rstd", [P, 2 * Q], F32)
        shift = sb("shift", [P, 2 * Q], F32)
        h = sb("h", [P, Q * D], F32)
        hT = sb("hT", [P, Q * N], F32)
        wh = sb("wh", [P, Q * D], F32)
        relu_z = sb("relu_z", [P, Q * N], F32)
        neg_e = sb("neg_e", [P, Q * N], F32)
        neg_max = sb("neg_max", [P, 2, Q], F32)
        prob = sb("prob", [P, Q * N], F32)
        row_sum = sb("row_sum", [P, 2, Q], F32)
        inv_sum = sb("inv_sum", [P, Q], F32)
        probT = sb("probT", [P, Q * N], F32)
        v1m = sb("v1m", [P, Q * D], F32)
        exp_v = sb("exp_v", [P, Q * D], F32)
        pre = sb("pre", [P, Q * D], F32)
        pay = sb("pay", [P, 2, K, Q, ROW], F32)
        h2T = sb("h2T", [P, Q * N], F32)
        logits = sb("logits", [P, Q, E], F32)
        top = sb("top", [P, Q, 8], F32)
        top_i = sb("top_i", [P, Q, 8], U32)
        gap = sb("gap", [P, B], F32)
        chosen = sb("chosen", [P, K, Q, E], F32)
        chosen_h = sb("chosen_h", [P, Q, E], F16)
        group_n = sb("group_n", [P, E], F32)
        count = sb("count", [P, E], F16)
        rank_of = sb("rank_of", [P, K, Q, E], F32)
        pos_f = sb("pos_f", [P, K, Q], F32)
        pos = sb("pos", [P, 2, K, Q], I32)
        gate = sb("gate", [P, K, B], F32)
        exp_gap = sb("exp_gap", [P, B], F32)
        gden = sb("gden", [P, B], F32)
        end_f = sb("end_f", [P, E], F32)
        end_i = sb("end_i", [P, E], I32)
        cnt_i = sb("cnt_i", [P, E], I32)
        ntile_i = sb("ntile_i", [P, E], I32)
        ntile_f = sb("ntile_f", [P, E], F32)
        ones_e = sb("ones_e", [P, E], F32)
        last_tile = sb("last_tile", [P, E], F32)
        skip = sb("skip", [P, E], F32)
        passed = sb("passed", [P, U, E], F32)
        passed_skip = sb("passed_skip", [P, U, E], F32)
        tab = sb("tab", [P, 2, U], F32)
        tab2 = sb("tab2", [P, 2, U], F32)
        tab3 = sb("tab3", [P, 2, U], F32)
        table_e = sb("table_e", [U, P], I32)
        table_r = sb("table_r", [U, P], I32)
        rows = sb("rows", [P, U, ROW], F32)
        xT = sb("xT", [P, 2, P], F32)
        silu = sb("silu", [P, 2, H], F32)
        hid = sb("hid", [P, 2, H], F32)
        hidT = sb("hidT", [P, 2, H], F32)
        y = sb("y", [P, U, D], F32)
        S = 4
        res = sb("res", [P, S, K, Q * D], F32)

        X_STARTS = [0, 1, 3]
        X_COUNTS = [1, 2, GROUPS - 3]
        x_in = [sem(f"x_in{i}") for i in range(3)]
        small_in = sem("small_in")
        adj_in = [sem(f"adj_in{i}") for i in range(2)]
        w_in = sem("w_in")
        scattered = [sem(f"scattered{i}") for i in range(2)]
        filled = sem("filled")
        rows_in = [sem(f"rows_in{i}") for i in range(U)]
        y_out = [sem(f"y_out{i}") for i in range(U)]
        res_in = [sem(f"res_in{i}") for i in range(S)]
        out_done = sem("out_done")
        pool_const = sem("pool_const")
        dve_const = sem("dve_const")
        gwT_done = sem("gwT_done")
        gwT_copied = sem("gwT_copied")
        a_spread = sem("a_spread")
        wa_done = sem("wa_done")
        wa_copied = sem("wa_copied")
        mask_done = sem("mask_done")
        stats_done = sem("stats_done")
        rs_done = sem("rs_done")
        h_done = sem("h_done")
        hT_done = sem("hT_done")
        hT_copied = sem("hT_copied")
        z_done = sem("z_done")
        wh_done = sem("wh_done")
        relu_done = sem("relu_done")
        wh_copied = sem("wh_copied")
        e_done = sem("e_done")
        prob_done = sem("prob_done")
        pT_done = sem("pT_done")
        pT_copied = sem("pT_copied")
        o_done = sem("o_done")
        v_done = sem("v_done")
        exp_done = sem("exp_done")
        x2_done = sem("x2_done")
        pay0_done = sem("pay0_done")
        pay1_done = sem("pay1_done")
        h2T_done = sem("h2T_done")
        h2T_copied = sem("h2T_copied")
        logit_done = sem("logit_done")
        chosen_done = sem("chosen_done")
        rank_done = sem("rank_done")
        count_done = sem("count_done")
        pos_done = sem("pos_done")
        ln_done = sem("ln_done")
        rs1_done = sem("rs1_done")
        rs2_done = sem("rs2_done")
        r_done = sem("r_done")
        rstd_done = sem("rstd_done")
        x_stats_done = sem("x_stats_done")
        x2_stats_done = sem("x2_stats_done")
        inv_done = sem("inv_done")
        pre_done = sem("pre_done")
        logit_copied = sem("logit_copied")
        top_done = sem("top_done")
        top_i_done = sem("top_i_done")
        gap_done = sem("gap_done")
        each_chosen = sem("each_chosen")
        group_n_done = sem("group_n_done")
        rank_of_done = sem("rank_of_done")
        pos_f_done = sem("pos_f_done")
        total_done = sem("total_done")
        end_done = sem("end_done")
        tab_step = sem("tab_step")
        tab_done = sem("tab_done")
        gate_step = sem("gate_step")
        tabT_done = sem("tabT_done")
        table_done = sem("table_done")
        gap_exp = sem("gap_exp")
        xT_done = sem("xT_done")
        xT_copied = sem("xT_copied")
        mlp_done = sem("mlp_done")
        silu_done = sem("silu_done")
        hid_done = sem("hid_done")
        hidT_done = sem("hidT_done")
        hidT_copied = sem("hidT_copied")
        y_done = sem("y_done")
        y_copied = sem("y_copied")
        gated_done = sem("gated_done")
        both_done = sem("both_done")
        sum_done = sem("sum_done")

        def wait(eng, s, value):
            if not isinstance(value, int) or value > 0:
                eng.wait_ge(s, value)

        def wait_apart(eng, *counts):
            counts = [(s, n if isinstance(n, int) else eng.to_reg(n)) for s, n in counts]
            eng.wait_ge(pool_const, 2)
            for s, n in counts:
                wait(eng, s, n)

        def valid(n, end):
            return not isinstance(n, int) or 0 <= n < end

        def iterations(eng, body):
            for it in range(-2, 4):
                body(it, it % 2)
            with eng.Fori(0, (GROUPS - 6) // 2) as trip:
                body(trip * 2 + 4, 0)
                body(trip * 2 + 5, 1)
            for it in range(GROUPS - 2, GROUPS + 3):
                body(it, it % 2)

        def tiles(eng, body):
            body(-1, U - 2)
            body(-1, U - 1)
            for j in range(U):
                body(0, j)
            with eng.Fori(1, TILES // U - 1) as trip:
                for j in range(U):
                    body(trip, j)
            for j in range(U):
                body(TILES // U - 1, j)
            for j in range(2):
                body(TILES // U, j)

        def tile_at(trip, j, ahead):
            trip, j = trip + (j + ahead) // U, (j + ahead) % U
            return trip * U + j, trip, j

        def slot_sent(g, slot):
            return 8 * K * Q * (g - slot)

        def cols(t, g, n=Q * D):
            return t[:, bass.ds(g * n, n)]

        block = ctx.enter_context(nc.Block())

        @block.sync
        def _(sp):
            x_v = x.rearrange("b n f -> n b f")
            adj_v = adj.rearrange("b n m -> n b m")

            def load_x(g):
                sp.dma_start(x_all[:, g * Q * D:(g + 1) * Q * D].rearrange("p (q f) -> p q f", q=Q),
                             x_v[:, g * Q:(g + 1) * Q, :]).then_inc(x_in[sum(g >= n for n in X_STARTS[1:])], 16)

            def load_weights(e):
                sp.dma_start(w12[:, bass.ds(e * (2 * H), H)], w1[bass.ds(e, 1), :, :].rearrange("e d h -> (e d) h"))\
                    .then_inc(w_in, 16)
                sp.dma_start(w12[:, bass.ds(e * (2 * H) + H, H)], w2[bass.ds(e, 1), :, :].rearrange("e d h -> (e d) h"))\
                    .then_inc(w_in, 16)
                sp.dma_start(w3s[:, bass.ds(e * (2 * D), 2 * D)].rearrange("p (c d) -> p c d", c=2),
                             w3[bass.ds(e, 1), :, :].rearrange("e (c p) d -> p (e c) d", c=2)).then_inc(w_in, 16)

            def load_adj(g, slot):
                wait(sp, mask_done, g - 1)
                sp.dma_start(adj_s[:, slot, :].rearrange("p (q m) -> p q m", q=Q),
                             adj_v[:, bass.ds(g * Q, Q), :]).then_inc(adj_in[slot], 16)

            load_x(0)
            sp.dma_start(gw[:, :], gnn_w).then_inc(small_in, 16)
            sp.dma_start(a_col[:, :], gnn_a.rearrange("(k f) o -> f (k o)", k=2),
                         allow_slow_non_contiguous=True).then_inc(small_in, 16)
            load_adj(0, 0)
            load_x(1)
            load_adj(1, 1)
            sp.dma_start(gate_ws[:, :], gate_w).then_inc(small_in, 16)
            for q in range(Q):
                sp.dma_start(bias_row[:, q, :], gate_b.rearrange("(a e) -> a e", a=1)).then_inc(small_in, 16)
            for g in range(2, GROUPS):
                load_x(g)
            assert E == GROUPS
            load_weights(0)
            load_weights(1)
            with sp.Fori(1, GROUPS // 2) as pair:
                for s in range(2):
                    load_adj(pair * 2 + s, s)
                    load_weights(pair * 2 + s)

            sp.wait_ge(pool_const, 1)
            sp.wait_ge(dve_const, 1)
            sp.dma_start(rows_dram[E * REGION:E * REGION + P, :], zero_rows[:, :]).then_inc(filled, 16)
            sp.wait_ge(end_done, 1)
            with sp.Fori(0, E // 2) as e:
                end = sp.value_load(end_i[0:1, bass.ds(e, 1)], min_val=0, max_val=E * REGION - P)
                sp.dma_start(rows_dram[bass.ds(end, P), :], zero_rows[:, :]).then_inc(filled, 16)

            for s in scattered:
                sp.wait_ge(s, 16 * K * Q * GROUPS // 2)
            sp.wait_ge(filled, 16 * (E + 1))
            sp.wait_ge(table_done, 1)

            def load_rows(trip, j):
                first = sp.value_load(table_r[j:j + 1, bass.ds(trip, 1)], min_val=0, max_val=E * REGION)
                wait(sp, y_out[j], trip * 16)
                sp.dma_start(rows[:, j, :], rows_dram[bass.ds(first, P), :]).then_inc(rows_in[j], 16)

            for j in range(U):
                load_rows(0, j)
            with sp.Fori(1, TILES // U) as trip:
                for j in range(U):
                    load_rows(trip, j)

            for s in y_out:
                sp.wait_ge(s, 16 * TILES // U)
            res_v = result_dram.rearrange("(k b n) d -> n k b d", k=K, n=N)

            def load_res(g, s):
                wait(sp, sum_done, g - S + 1)
                for k in range(K):
                    sp.dma_start(res[:, s, k, :].rearrange("p (q d) -> p q d", q=Q),
                                 res_v[:, k, bass.ds(g * Q, Q), :]).then_inc(res_in[s], 16)

            for s in range(S):
                load_res(s, s)
            with sp.Fori(1, GROUPS // S) as trip:
                for s in range(S):
                    load_res(trip * S + s, s)
            sp.wait_ge(out_done, 16 * GROUPS)

        @block.gpsimd
        def _(pool):
            nc.gpsimd.memset(ident[:, :], 0.0)
            nc.gpsimd.memset(ones_h[:, :], 1.0)
            nc.gpsimd.memset(before[:, :], 1.0).then_inc(pool_const, 1)
            pool.wait_ge(pool_const, 1)
            nc.gpsimd.affine_select(out=ident[:, :], in_=ident[:, :], compare_op=ALU.not_equal, fill=1.0,
                                    base=0, pattern=[[-1, P]], channel_multiplier=1)
            nc.gpsimd.affine_select(out=before[:, :], in_=before[:, :], compare_op=ALU.is_gt, fill=0.0,
                                    base=0, pattern=[[1, P]], channel_multiplier=-1)
            nc.gpsimd.iota(expert_no[:, :], [[1, E]], base=0, channel_multiplier=0,
                           allow_small_or_imprecise_dtypes=True)
            nc.gpsimd.iota(tile_no[:, :], [[1, U]], base=0, channel_multiplier=U,
                           allow_small_or_imprecise_dtypes=True)
            nc.gpsimd.iota(dest_all[:, :, :], [[TOKENS, K], [N, B]], base=0, channel_multiplier=1)
            nc.gpsimd.iota(count[:, :], [[COUNT_BASE, E]], base=0, channel_multiplier=0,
                           allow_small_or_imprecise_dtypes=True).then_inc(pool_const, 1)

            def scatter(g, slot):
                wait_apart(pool, (pos_done, g + 1),
                           (pay1_done, g + 1))
                for k in range(K):
                    for q in range(Q):
                        nc.gpsimd.indirect_dma_start(
                            out=rows_dram, out_offset=bass.IndirectOffsetOnAxis(
                                ap=pos[:, slot, k, q:q + 1].bitcast(U32), axis=0),
                            in_=pay[:, slot, k, q, :], in_offset=None,
                        ).then_inc(scattered[slot], 16)

            with pool.Fori(0, GROUPS // 2) as pair:
                scatter(pair * 2, 0)
                scatter(pair * 2 + 1, 1)

            def send_y(trip, j):
                wait_apart(pool, (y_copied, trip * U + (j + 1)))
                nc.gpsimd.indirect_dma_start(
                    out=result_dram, out_offset=bass.IndirectOffsetOnAxis(
                        ap=rows[:, j, D:D + 1].bitcast(U32), axis=0),
                    in_=y[:, j, :], in_offset=None, bounds_check=NOWHERE - 1, oob_is_err=False,
                ).then_inc(y_out[j], 16)

            with pool.Fori(0, TILES // U) as trip:
                for j in range(U):
                    send_y(trip, j)

            with pool.Fori(0, GROUPS // S) as trip:
                for s in range(S):
                    pool.wait_ge(gated_done, trip * S + (s + 1))
                    nc.gpsimd.tensor_tensor(res[:, s, 0, :], res[:, s, 0, :], res[:, s, 1, :], ALU.add)\
                        .then_inc(both_done, 1)

        @block.tensor
        def _(pe):
            pe.wait_ge(pool_const, 2)
            pe.wait_ge(small_in, 16 * (3 + Q))
            nc.tensor.transpose(hT_ps[:, 0:P], gw[:, :], ident[:, :]).then_inc(gwT_done, 1)
            pe.wait_ge(gwT_copied, 1)
            pe.wait_ge(a_spread, 1)
            for k in range(2):
                last = nc.tensor.matmul(z_ps[:, k * P:(k + 1) * P], gwT[:, :], a_rep[:, k, :], start=True, stop=True)
            last.then_inc(wa_done, 1)
            pe.wait_ge(wa_copied, 1)

            def body(it, s):
                g = it
                if valid(g, GROUPS):
                    pe.wait_ge(h_done, g + 1)
                    wait(pe, hT_copied, g)
                    for q in range(Q):
                        last = nc.tensor.transpose(hT_ps[:, q * N:(q + 1) * N], h[:, q * D:(q + 1) * D], ident[:, :])
                    last.then_inc(hT_done, 1)
                g = it - 1
                if valid(g, GROUPS):
                    pe.wait_ge(prob_done, g + 1)
                    wait(pe, pT_copied, g)
                    for q in range(Q):
                        last = nc.tensor.transpose(pT_ps[:, q * N:(q + 1) * N], prob[:, q * N:(q + 1) * N], ident[:, :])
                    last.then_inc(pT_done, 1)
                g = it - 3
                if valid(g, GROUPS):
                    pe.wait_ge(chosen_done, g + 1)
                    wait(pe, count_done, g)
                    wait(pe, rank_of_done, g)
                    nc.tensor.matmul(rank_ps[:, 0:Q * E], before[:, :], chosen_h[:, :, :], start=True, stop=False,
                                     skip_group_check=True)
                    for q in range(Q):
                        last = nc.tensor.matmul(rank_ps[:, q * E:(q + 1) * E], ones_h[:, :], count[:, :],
                                                start=False, stop=False, skip_group_check=True)
                        for r in range(q):
                            last = nc.tensor.matmul(rank_ps[:, q * E:(q + 1) * E], ones_h[:, :], chosen_h[:, r, :],
                                                    start=False, stop=(q == Q - 1 and r == q - 1),
                                                    skip_group_check=True)
                    last.then_inc(rank_done, 1)
                g = it
                if valid(g, GROUPS):
                    pe.wait_ge(hT_copied, g + 1)
                    wait(pe, e_done, g)
                    nc.tensor.matmul(z_ps[:, :], wa_rep[:, 1, :], hT[:, :], start=True, stop=False,
                                     skip_group_check=True)
                g = it - 1
                if valid(g, GROUPS):
                    pe.wait_ge(pT_copied, g + 1)
                    pe.wait_ge(wh_copied, g + 1)
                    wait(pe, v_done, g)
                    for q in range(Q):
                        last = nc.tensor.matmul(o_ps[:, q * D:(q + 1) * D], probT[:, q * N:(q + 1) * N],
                                                wh[:, q * D:(q + 1) * D], start=True, stop=True)
                    last.then_inc(o_done, 1)
                g = it
                if valid(g, GROUPS):
                    pe.wait_ge(mask_done, g + 1)
                    for q in range(Q):
                        nc.tensor.matmul(z_ps[:, q * N:(q + 1) * N], hT[:, q * N:(q + 1) * N], wa_rep[:, 0, :],
                                         start=False, stop=False, skip_group_check=True)
                    nc.tensor.matmul(z_ps[:, :], ident_b[:, :], mask[:, s, :], start=False, stop=True,
                                     skip_group_check=True).then_inc(z_done, 1)
                g = it - 2
                if valid(g, GROUPS):
                    pe.wait_ge(pay0_done, g + 1)
                    wait(pe, h2T_copied, g)
                    for q in range(Q):
                        last = nc.tensor.transpose(h2T_ps[:, q * N:(q + 1) * N], pay[:, s, 0, q, 0:D], ident[:, :])
                    last.then_inc(h2T_done, 1)
                g = it
                if valid(g, GROUPS):
                    wait(pe, wh_copied, g)
                    for q in range(Q):
                        last = nc.tensor.matmul(wh_ps[:, q * D:(q + 1) * D], hT[:, q * N:(q + 1) * N], gw[:, :],
                                                start=True, stop=True)
                    last.then_inc(wh_done, 1)
                g = it - 2
                if valid(g, GROUPS):
                    pe.wait_ge(h2T_copied, g + 1)
                    wait(pe, logit_copied, g)
                    nc.tensor.matmul(logit_ps[:, 0:Q * E], ones_row[:, :], bias_row[:, :, :], start=True, stop=False,
                                     skip_group_check=True)
                    for q in range(Q):
                        last = nc.tensor.matmul(logit_ps[:, q * E:(q + 1) * E], h2T[:, q * N:(q + 1) * N],
                                                gate_ws[:, :], start=False, stop=(q == Q - 1), skip_group_check=True)
                    last.then_inc(logit_done, 1)

            iterations(pe, body)

            pe.wait_ge(count_done, GROUPS)
            pe.wait_ge(pos_done, GROUPS)
            nc.tensor.matmul(rank_ps[:, 0:E], ones_h[:, :], count[:, :], start=True, stop=True).then_inc(total_done, 1)
            pe.wait_ge(tab_done, 1)
            for k in range(2):
                last = nc.tensor.transpose(logit_ps[0:U, k * P:(k + 1) * P], tab3[:, k, :], ident[:, :])
            last.then_inc(tabT_done, 1)

            pe.wait_ge(table_done, 1)
            pe.wait_ge(w_in, 48 * E)

            expert_reg = [pe.alloc_register(f"expert{j}") for j in range(U)]

            def load_expert(trip, j):
                pe.reg_load(expert_reg[j], table_e[j:j + 1, bass.ds(trip, 1)])

            def expert(j):
                return pe.snap(expert_reg[j], min_val=0, max_val=E - 1)

            load_expert(0, 0)

            def tile(trip, j):
                n, tr, m = tile_at(trip, j, 0)
                if valid(n, TILES):
                    e = expert(m)
                    pe.wait_ge(xT_copied, n + 1)
                    wait(pe, hid_done, n - 1)
                    nc.tensor.matmul(mlp_ps[m % 2][:, :], xT[:, m % 2, :], w12[:, bass.ds(e * (2 * H), 2 * H)],
                                     start=True, stop=True).then_inc(mlp_done, 1)
                n, tr, m = tile_at(trip, j, 1)
                if valid(n, TILES) and not (isinstance(n, int) and n == 0):
                    load_expert(tr, m)
                n, tr, m = tile_at(trip, j, 2)
                if valid(n, TILES):
                    pe.wait_ge(rows_in[m], tr * 16 + 16)
                    wait(pe, xT_copied, n - 1)
                    nc.tensor.transpose(xT_ps[m % 2][:, 0:P], rows[:, m, 0:D], ident[:, :]).then_inc(xT_done, 1)
                n, tr, m = tile_at(trip, j, -1)
                if valid(n, TILES):
                    pe.wait_ge(hid_done, n + 1)
                    wait(pe, hidT_copied, n - 1)
                    for c in range(2):
                        last = nc.tensor.transpose(gT_ps[m % 2][:, c * P:(c + 1) * P],
                                                   hid[:, m % 2, c * P:(c + 1) * P], ident[:, :])
                    last.then_inc(hidT_done, 1)
                n, tr, m = tile_at(trip, j, -2)
                if valid(n, TILES):
                    e = expert(m)
                    pe.wait_ge(hidT_copied, n + 1)
                    wait(pe, y_copied, n - 1)
                    for c in range(2):
                        last = nc.tensor.matmul(y_ps[m % 2][:, 0:D], hidT[:, m % 2, c * P:(c + 1) * P],
                                                w3s[:, bass.ds(e * (2 * D) + c * D, D)], start=(c == 0), stop=(c == 1))
                    last.then_inc(y_done, 1)

            tiles(pe, tile)

        @block.scalar
        def _(act):
            act.wait_ge(gwT_done, 1)
            nc.scalar.activation(gwT[:, :], hT_ps[:, 0:P], ACT.Copy).then_inc(gwT_copied, 1)
            act.wait_ge(wa_done, 1)
            nc.scalar.activation(wa_rep[:, :, :], z_ps[:, 0:2 * P], ACT.Copy).then_inc(wa_copied, 1)

            nc.scalar.preload_act_table_set("natural_log_exp_and_others")

            def body(it, s):
                g = it - 1
                if valid(g, GROUPS):
                    act.wait_ge(e_done, g + 1)
                    wait(act, pT_done, g)
                    for q in range(Q):
                        last = nc.scalar.activation(prob[:, q * N:(q + 1) * N], neg_e[:, q * N:(q + 1) * N], ACT.Exp,
                                                    bias=neg_max[:, 1 - s, q:q + 1], scale=-1.0,
                                                    accum_out=row_sum[:, 1 - s, q:q + 1])
                    last.then_inc(prob_done, 1)
                g = it
                if valid(g, GROUPS):
                    act.wait_ge(hT_done, g + 1)
                    wait(act, wh_done, g)
                    nc.scalar.activation(hT[:, :], hT_ps[:, :], ACT.Copy).then_inc(hT_copied, 1)
                g = it - 1
                if valid(g, GROUPS):
                    act.wait_ge(wh_done, g + 1)
                    wait(act, o_done, g)
                    nc.scalar.activation(wh[:, :], wh_ps[:, :], ACT.Copy, bias=-1.0).then_inc(wh_copied, 1)
                    act.wait_ge(pT_done, g + 1)
                    nc.scalar.activation(probT[:, :], pT_ps[:, :], ACT.Copy).then_inc(pT_copied, 1)
                g = it - 2
                if valid(g, GROUPS):
                    counts = [(rstd_done, g + 4)]
                    if not isinstance(g, int) or g >= 2:
                        counts += [(scattered[s], slot_sent(g, s))]
                    wait_apart(act, *counts)
                    for q in range(Q):
                        last = nc.scalar.activation(pay[:, s, 0, q, 0:D], x_all[:, bass.ds(g * (Q * D) + q * D, D)],
                                                    ACT.Identity, bias=shift[:, q:q + 1], scale=rstd[:, q:q + 1])
                    last.then_inc(pay0_done, 1)
                g = it - 1
                if valid(g, GROUPS):
                    act.wait_ge(v_done, g + 1)
                    wait(act, x2_done, g)
                    nc.scalar.activation(exp_v[:, :], v1m[:, :], ACT.Exp, bias=ones_e[:, 0:1]).then_inc(exp_done, 1)
                g = it
                if valid(g, GROUPS):
                    act.wait_ge(z_done, g + 1)
                    wait(act, e_done, g)
                    nc.scalar.activation(relu_z[:, :], z_ps[:, :], ACT.Relu, scale=1 / ALPHA - 1).then_inc(relu_done, 1)
                g = it - 2
                if valid(g, GROUPS):
                    act.wait_ge(h2T_done, g + 1)
                    wait(act, logit_done, g)
                    nc.scalar.activation(h2T[:, :], h2T_ps[:, :], ACT.Copy).then_inc(h2T_copied, 1)
                g = it + 1
                if valid(g, GROUPS):
                    wait_apart(act, (rstd_done, g + 1),
                               (hT_done, g))
                    for q in range(Q):
                        last = nc.scalar.activation(h[:, q * D:(q + 1) * D], x_all[:, bass.ds(g * (Q * D) + q * D, D)],
                                                    ACT.Identity, bias=shift[:, Q + q:Q + q + 1],
                                                    scale=rstd[:, Q + q:Q + q + 1])
                    last.then_inc(h_done, 1)
                if valid(it + 2, GROUPS) or valid(it - 1, GROUPS):
                    n = it + 3
                    act.wait_ge(stats_done, n)
                    nc.scalar.activation(lnv[:, :], mv[:, :, 1], ACT.Ln, bias=eps_col[:, 0:1]).then_inc(ln_done, 1)
                    act.wait_ge(ln_done, n)
                    nc.scalar.activation(rs0[:, :], lnv[:, :], ACT.Exp, scale=-0.5).then_inc(rs_done, 1)

            iterations(act, body)
            act.wait_ge(end_done, 1)
            with act.Fori(E // 2, E) as e:
                end = act.value_load(end_i[0:1, bass.ds(e, 1)], min_val=0, max_val=E * REGION - P)
                act.dma_start(rows_dram[bass.ds(end, P), :], zero_rows[:, :]).then_inc(filled, 16)
            act.wait_ge(gap_done, GROUPS)
            nc.scalar.activation(exp_gap[:, :], gap[:, :], ACT.Exp).then_inc(gap_exp, 1)

            def tile(trip, j):
                n, tr, m = tile_at(trip, j, 0)
                if valid(n, TILES):
                    act.wait_ge(mlp_done, n + 1)
                    wait(act, hid_done, n - 1)
                    nc.scalar.activation(silu[:, m % 2, :], mlp_ps[m % 2][:, 0:H], ACT.Silu).then_inc(silu_done, 1)
                n, tr, m = tile_at(trip, j, 2)
                if valid(n, TILES):
                    act.wait_ge(xT_done, n + 1)
                    wait(act, mlp_done, n - 1)
                    nc.scalar.activation(xT[:, m % 2, :], xT_ps[m % 2][:, 0:P], ACT.Copy).then_inc(xT_copied, 1)
                n, tr, m = tile_at(trip, j, -2)
                if valid(n, TILES):
                    act.wait_ge(y_done, n + 1)
                    wait(act, y_out[m], tr * 16)
                    nc.scalar.activation(y[:, m, :], y_ps[m % 2][:, 0:D], ACT.Copy).then_inc(y_copied, 1)

            tiles(act, tile)

            out_v = out.rearrange("b n f -> n b f")
            with act.Fori(0, GROUPS) as g:
                act.wait_ge(sum_done, g + 1)
                act.dma_start(out_v[:, bass.ds(g * Q, Q), :],
                              cols(x_all, g).rearrange("p (q f) -> p q f", q=Q)).then_inc(out_done, 16)

        @block.vector
        def _(dve):
            nc.vector.memset(eps_col[:, :], EPS)
            nc.vector.memset(ones_row[:, :], 1.0)
            nc.vector.memset(ones_e[:, :], 1.0)
            nc.vector.memset(mv[:, :, :], 1.0)
            nc.vector.memset(pay[:, :, :, :, :], 0.0)
            nc.vector.memset(zero_rows[:, 0:D], 0.0)
            nc.vector.memset(zero_rows[:, D:ROW].bitcast(I32), NOWHERE).then_inc(dve_const, 1)
            dve.wait_ge(pool_const, 2)
            nc.vector.tensor_copy(ident_b[:, :], ident[:, :])
            nc.vector.tensor_scalar(region_no[:, :], expert_no[:, :], float(REGION), None, ALU.mult)
            dve.wait_ge(small_in, 16 * (3 + Q))
            for k in range(2):
                last = nc.vector.tensor_copy(a_rep[:, k, :], a_col[:, k:k + 1].to_broadcast([P, P]))
            last.then_inc(a_spread, 1)

            def body(it, s):
                g = it - 3
                if valid(g, GROUPS):
                    dve.wait_ge(logit_done, g + 1)
                    nc.vector.tensor_copy(logits[:, :, :], logit_ps[:, 0:Q * E]).then_inc(logit_copied, 1)
                n = it + 2
                if valid(n, GROUPS):
                    for part, start in enumerate(X_STARTS):
                        if isinstance(n, int) and n == start:
                            dve.wait_ge(x_in[part], 16 * X_COUNTS[part])
                    wait_apart(dve, (stats_done, n))
                    for q in range(Q):
                        last = nc.vector.bn_stats(x_stats[:, q, :], x_all[:, bass.ds(n * (Q * D) + q * D, D)])
                    last.then_inc(x_stats_done, 1)
                g = it - 3
                if valid(g, GROUPS):
                    wait_apart(dve, (logit_copied, g + 1))
                    for q in range(Q):
                        last = nc.vector.max(top[:, q, :], logits[:, q, :])
                    last.then_inc(top_done, 1)
                newton = valid(it + 1, GROUPS) or valid(it - 2, GROUPS)
                if newton:
                    dve.wait_ge(rs_done, it + 2)
                    nc.vector.scalar_tensor_tensor(rs1[:, :], mv[:, :, 1], EPS, rs0[:, :], ALU.add, ALU.mult)\
                        .then_inc(rs1_done, 1)
                g = it - 3
                if valid(g, GROUPS):
                    wait_apart(dve, (top_done, g + 1))
                    for q in range(Q):
                        last = nc.vector.max_index(top_i[:, q, :], top[:, q, :], logits[:, q, :])
                    last.then_inc(top_i_done, 1)
                if newton:
                    dve.wait_ge(rs1_done, it + 2)
                    nc.vector.scalar_tensor_tensor(rs2[:, :], rs1[:, :], -0.5, rs0[:, :], ALU.mult, ALU.mult)\
                        .then_inc(rs2_done, 1)
                g = it - 3
                if valid(g, GROUPS):
                    nc.vector.tensor_tensor(gap[:, bass.ds(g * Q, Q)], top[:, :, 1], top[:, :, 0], ALU.subtract)\
                        .then_inc(gap_done, 1)
                    dve.wait_ge(top_i_done, g + 1)
                    nc.vector.tensor_tensor(
                        chosen[:, :, :, :],
                        expert_no[:, :].unsqueeze(1).unsqueeze(1).to_broadcast([P, K, Q, E]),
                        top_i[:, :, 0:K].rearrange("p q k -> p k q").unsqueeze(3).to_broadcast([P, K, Q, E]),
                        ALU.is_equal).then_inc(each_chosen, 1)
                if newton:
                    dve.wait_ge(rs2_done, it + 2)
                    wait(dve, pay0_done, it - 2)
                    if valid(it, GROUPS):
                        wait(dve, h_done, it + 1)
                    nc.vector.scalar_tensor_tensor(rstd[:, :], rs2[:, :], 1.5, rs0[:, :], ALU.add, ALU.mult)\
                        .then_inc(r_done, 1)
                g = it - 3
                if valid(g, GROUPS):
                    dve.wait_ge(each_chosen, g + 1)
                    wait(dve, rank_done, g)
                    nc.vector.tensor_tensor(chosen_h[:, :, :], chosen[:, 0, :, :], chosen[:, 1, :, :], ALU.add)\
                        .then_inc(chosen_done, 1)
                if newton:
                    dve.wait_ge(r_done, it + 2)
                    nc.vector.scalar_tensor_tensor(shift[:, :], mv[:, :, 0], -1.0, rstd[:, :], ALU.mult, ALU.mult)\
                        .then_inc(rstd_done, 1)
                n = it + 1
                if valid(n, GROUPS):
                    dve.wait_ge(adj_in[1 - s], (n - (1 - s)) * 8 + 16)
                    wait(dve, z_done, n - 1)
                    nc.vector.tensor_scalar(mask[:, 1 - s, :], adj_s[:, 1 - s, :], 0, NEG_BIG, ALU.is_le, ALU.mult)\
                        .then_inc(mask_done, 1)
                g = it - 3
                if valid(g, GROUPS):
                    dve.wait_ge(chosen_done, g + 1)
                    nc.vector.tensor_reduce(group_n[:, :], chosen_h[:, :, :].rearrange("p q e -> p e q"),
                                            AX_X, ALU.add).then_inc(group_n_done, 1)
                    dve.wait_ge(rank_done, g + 1)
                    nc.vector.tensor_tensor(
                        rank_of[:, :, :, :],
                        rank_ps[:, 0:Q * E].rearrange("p (q e) -> p q e", q=Q).unsqueeze(1).to_broadcast([P, K, Q, E]),
                        chosen[:, :, :, :], ALU.mult).then_inc(rank_of_done, 1)
                    dve.wait_ge(group_n_done, g + 1)
                    nc.vector.tensor_tensor(count[:, :], count[:, :], group_n[:, :], ALU.add).then_inc(count_done, 1)
                    dve.wait_ge(rank_of_done, g + 1)
                    nc.vector.tensor_reduce(pos_f[:, :, :], rank_of[:, :, :, :], AX_X, ALU.add).then_inc(pos_f_done, 1)
                n = it + 2
                if valid(n, GROUPS):
                    wait_apart(dve, (x_stats_done, n + 1),
                               (rstd_done, it + 2))
                    for q in range(Q):
                        last = nc.vector.bn_aggr(mv[:, Q + q, :], x_stats[:, q, :])
                    if not valid(it - 1, GROUPS):
                        last.then_inc(stats_done, 1)
                g = it - 3
                if valid(g, GROUPS):
                    dve.wait_ge(pos_f_done, g + 1)
                    nc.vector.tensor_copy(pos[:, 1 - s, :, :], pos_f[:, :, :]).then_inc(pos_done, 1)
                g = it - 1
                if valid(g, GROUPS):
                    xg = cols(x_all, g)
                    dve.wait_ge(prob_done, g + 1)
                    nc.vector.reciprocal(inv_sum[:, :], row_sum[:, 1 - s, :]).then_inc(inv_done, 1)
                    dve.wait_ge(o_done, g + 1)
                    dve.wait_ge(inv_done, g + 1)
                    wait(dve, exp_done, g)
                    nc.vector.tensor_tensor(v1m[:, :].rearrange("p (q d) -> p q d", q=Q),
                                            o_ps[:, :].rearrange("p (q d) -> p q d", q=Q),
                                            inv_sum[:, :].unsqueeze(2).to_broadcast([P, Q, D]),
                                            ALU.mult).then_inc(v_done, 1)
                    dve.wait_ge(v_done, g + 1)
                    nc.vector.scalar_tensor_tensor(pre[:, :], v1m[:, :], -1.0, xg, ALU.max, ALU.add).then_inc(pre_done, 1)
                g = it - 2
                if valid(g, GROUPS):
                    dve.wait_ge(pay0_done, g + 1)
                    nc.vector.tensor_copy(pay[:, s, 1, :, 0:D], pay[:, s, 0, :, 0:D])
                    nc.vector.tensor_copy(pay[:, s, :, :, D].bitcast(I32), dest_all[:, :, bass.ds(g * Q, Q)])\
                        .then_inc(pay1_done, 1)
                g = it - 1
                if valid(g, GROUPS):
                    dve.wait_ge(exp_done, g + 1)
                    dve.wait_ge(pre_done, g + 1)
                    nc.vector.scalar_tensor_tensor(xg, exp_v[:, :], 1.0, pre[:, :], ALU.min, ALU.add)\
                        .then_inc(x2_done, 1)
                    wait_apart(dve, (x2_done, g + 1))
                    for q in range(Q):
                        last = nc.vector.bn_stats(x2_stats[:, q, :], x_all[:, bass.ds(g * (Q * D) + q * D, D)])
                    last.then_inc(x2_stats_done, 1)
                    wait_apart(dve, (x2_stats_done, g + 1),
                               (rstd_done, it + 2))
                    for q in range(Q):
                        last = nc.vector.bn_aggr(mv[:, q, :], x2_stats[:, q, :])
                    last.then_inc(stats_done, 1)
                g = it
                if valid(g, GROUPS):
                    wait_apart(dve, (relu_done, g + 1),
                               (prob_done, g))
                    for q in range(Q):
                        last = nc.vector.tensor_tensor_reduce(
                            neg_e[:, q * N:(q + 1) * N], z_ps[:, q * N:(q + 1) * N], relu_z[:, q * N:(q + 1) * N],
                            -ALPHA, 3.0e38, ALU.add, ALU.min, neg_max[:, s, q:q + 1])
                    last.then_inc(e_done, 1)

            iterations(dve, body)

            dve.wait_ge(total_done, 1)
            nc.vector.tensor_copy(end_i[:, :], rank_ps[:, 0:E]).then_inc(end_done, 1)
            nc.vector.scalar_tensor_tensor(cnt_i[:, :], rank_ps[:, 0:E], float(P - 1), region_no[:, :],
                                           ALU.add, ALU.subtract).then_inc(tab_step, 1)
            dve.wait_ge(tab_step, 1)
            nc.vector.tensor_scalar(ntile_i[:, :], cnt_i[:, :], 7, None, ALU.arith_shift_right).then_inc(tab_step, 1)
            dve.wait_ge(tab_step, 2)
            nc.vector.tensor_copy(ntile_f[:, :], ntile_i[:, :]).then_inc(tab_step, 1)
            dve.wait_ge(tab_step, 3)
            nc.vector.tensor_tensor_scan(last_tile[:, :], ones_e[:, :], ntile_f[:, :], 0.0, ALU.mult, ALU.add)
            nc.vector.tensor_scalar(skip[:, :], ntile_f[:, :], -float(P), float(REGION), ALU.mult, ALU.add)\
                .then_inc(tab_step, 1)
            dve.wait_ge(tab_step, 4)
            nc.vector.tensor_tensor(passed[:, :, :], tile_no[:, :].unsqueeze(2).to_broadcast([P, U, E]),
                                    last_tile[:, :].unsqueeze(1).to_broadcast([P, U, E]), ALU.is_ge)\
                .then_inc(tab_step, 1)
            dve.wait_ge(tab_step, 5)
            nc.vector.tensor_tensor(passed_skip[:, :, :], passed[:, :, :],
                                    skip[:, :].unsqueeze(1).to_broadcast([P, U, E]), ALU.mult)
            nc.vector.tensor_reduce(tab[:, 0, :], passed[:, :, :], AX_X, ALU.add).then_inc(tab_step, 1)
            dve.wait_ge(tab_step, 6)
            nc.vector.tensor_reduce(tab[:, 1, :], passed_skip[:, :, :], AX_X, ALU.add)
            nc.vector.tensor_scalar(tab3[:, 0, :], tab[:, 0, :], float(E - 1), None, ALU.min).then_inc(tab_step, 1)
            dve.wait_ge(tab_step, 7)
            nc.vector.scalar_tensor_tensor(tab2[:, 1, :], tile_no[:, :], float(P), tab[:, 1, :], ALU.mult, ALU.add)\
                .then_inc(tab_step, 1)
            dve.wait_ge(tab_step, 8)
            nc.vector.tensor_scalar(tab3[:, 1, :], tab2[:, 1, :], float(E * REGION), None, ALU.min).then_inc(tab_done, 1)
            dve.wait_ge(tabT_done, 1)
            nc.vector.tensor_copy(table_e[:, :], logit_ps[0:U, 0:P])
            nc.vector.tensor_copy(table_r[:, :], logit_ps[0:U, P:2 * P]).then_inc(table_done, 1)

            dve.wait_ge(gap_exp, 1)
            nc.vector.tensor_scalar(gden[:, :], exp_gap[:, :], 1.0, None, ALU.add).then_inc(gate_step, 1)
            dve.wait_ge(gate_step, 1)
            nc.vector.reciprocal(gate[:, 0, :], gden[:, :]).then_inc(gate_step, 1)
            dve.wait_ge(gate_step, 2)
            nc.vector.tensor_tensor(gate[:, 1, :], exp_gap[:, :], gate[:, 0, :], ALU.mult).then_inc(gate_step, 1)

            def tile(trip, j):
                n, tr, m = tile_at(trip, j, 0)
                if valid(n, TILES):
                    dve.wait_ge(silu_done, n + 1)
                    wait(dve, hidT_done, n - 1)
                    nc.vector.tensor_tensor(hid[:, m % 2, :], silu[:, m % 2, :], mlp_ps[m % 2][:, H:2 * H], ALU.mult)\
                        .then_inc(hid_done, 1)
                n, tr, m = tile_at(trip, j, -1)
                if valid(n, TILES):
                    dve.wait_ge(hidT_done, n + 1)
                    wait(dve, y_done, n - 1)
                    nc.vector.tensor_copy(hidT[:, m % 2, :], gT_ps[m % 2][:, 0:H]).then_inc(hidT_copied, 1)

            tiles(dve, tile)

            dve.wait_ge(gate_step, 3)

            def gate_results(trip, s):
                g = trip * S + s
                dve.wait_ge(res_in[s], trip * 32 + 32)
                r = res[:, s, :, :].rearrange("p k (q d) -> p k q d", q=Q)
                nc.vector.tensor_tensor(r, r, gate[:, :, bass.ds(g * Q, Q)].unsqueeze(3).to_broadcast([P, K, Q, D]),
                                        ALU.mult).then_inc(gated_done, 1)

            def add_results(g, s):
                dve.wait_ge(both_done, g + 1)
                nc.vector.tensor_tensor(cols(x_all, g), cols(x_all, g), res[:, s, 0, :], ALU.add).then_inc(sum_done, 1)

            for s in range(S):
                gate_results(0, s)
                if s > 0:
                    add_results(s - 1, s - 1)
            with dve.Fori(1, GROUPS // S) as trip:
                for s in range(S):
                    gate_results(trip, s)
                    add_results(trip * S + (s - 1), (s - 1) % S)
            add_results(GROUPS - 1, S - 1)


_INS = ["x", "adj", "L0_gnn_W", "L0_gnn_a", "L0_ffn_gate_w", "L0_ffn_gate_b", "L0_ffn_w1", "L0_ffn_w2", "L0_ffn_w3"]


def kernel(**inputs):
    import numpy as np
    import concourse.bacc as bacc
    from concourse.bass_utils import run_bass_kernel_spmd

    nc = bacc.Bacc("TRN2", target_bir_lowering=False, num_devices=1)
    arrays, args = {}, []
    for name in _INS:
        a = np.ascontiguousarray(inputs[name])
        arrays[f"in_{name}"] = a
        args.append(nc.dram_tensor(f"in_{name}", a.shape, mybir.dt.from_np(a.dtype), kind="ExternalInput").ap())
    x = arrays["in_x"]
    args.append(nc.dram_tensor("out", x.shape, mybir.dt.from_np(x.dtype), kind="ExternalOutput").ap())
    gnn_moe_kernel(nc, *args)
    r = run_bass_kernel_spmd(nc, [arrays], core_ids=[0])
    return r.results[0]["out"]
```

```python
from contextlib import ExitStack

import concourse.bass as bass
from concourse import mybir

F32 = mybir.dt.float32
F32R = mybir.dt.float32r
F16 = mybir.dt.float16
BF16 = mybir.dt.bfloat16
I32 = mybir.dt.int32
U32 = mybir.dt.uint32
ALU = mybir.AluOpType
ACT = mybir.ActivationFunctionType
AX_X = mybir.AxisListType.X

P = 128
EPS = 1e-5
ALPHA = 0.2
NEG_BIG = -9000000000000000.0


def gnn_moe_kernel(nc, x, adj, gnn_w, gnn_a, gate_w, gate_b, w1, w2, w3, out):
    B, N, D = x.shape
    E, _, H = w1.shape
    assert N == P and D == P and H == 2 * P and E == 16
    Q = 4
    GROUPS = B // Q
    TOKENS = B * N
    K = 2
    REGION = TOKENS + P
    assert REGION % P == 0
    NOWHERE = K * TOKENS
    ROW = D + 4
    U = 16
    TILES = -(-(K * TOKENS // P + E - 1) // U) * U
    COUNT_BASE = REGION // P

    rows_dram = nc.dram_tensor("dispatched_rows", [E * REGION + P, ROW], F32).ap()
    result_dram = nc.dram_tensor("expert_results", [K * TOKENS, D], F32).ap()

    ctx = ExitStack()
    with ctx:
        def sb(name, shape, dt):
            return ctx.enter_context(nc.sbuf_tensor(name, shape, dt))

        def sem(name):
            return ctx.enter_context(nc.semaphore(name))

        bank = [ctx.enter_context(nc.psum_tensor(f"bank{i}", [P, 512], F32)) for i in range(8)]
        hT_ps, z_ps, wh_ps, pT_ps, o_ps, h2T_ps, logit_ps, rank_ps = bank
        xT_ps, mlp_ps, gT_ps, y_ps = bank[0:2], bank[2:4], bank[4:6], bank[6:8]

        x_all = sb("x_all", [P, B * D], F32)
        W = 4 * H
        w12_split = sb("w12_split", [P, E * W], F32R)
        w12 = sb("w12", [P, 2, 2 * H], F32)
        w3s = sb("w3s", [P, E * 2 * D], F32)
        ident = sb("ident", [P, P], F32)
        ident_b = sb("ident_b", [P, P], BF16)
        before = sb("before", [P, P], F16)
        ones_h = sb("ones_h", [P, P], F16)
        ones_row = sb("ones_row", [1, P], F32)
        expert_no = sb("expert_no", [P, E], F32)
        dest_all = sb("dest_all", [P, K, B], I32)
        eps_col = sb("eps_col", [P, 1], F32)
        zero_rows = sb("zero_rows", [P, ROW], F32)
        tile_no = sb("tile_no", [P, U], F32)
        region_no = sb("region_no", [P, E], F32)
        gw = sb("gw", [P, D], F32)
        gwT = sb("gwT", [P, D], F32)
        a_col = sb("a_col", [P, 2], F32)
        a_rep = sb("a_rep", [P, 2, P], F32)
        wa_rep = sb("wa_rep", [P, 2, P], F32)
        gate_ws = sb("gate_ws", [P, E], F32)
        bias_row = sb("bias_row", [1, Q, E], F32)
        adj_s = sb("adj_s", [P, 2, Q * N], I32)
        mask = sb("mask", [P, 2, Q * N], BF16)
        x_stats = sb("x_stats", [P, Q, 6], F32)
        x2_stats = sb("x2_stats", [P, Q, 6], F32)
        mv = sb("mv", [P, 2 * Q, 2], F32)
        lnv = sb("lnv", [P, 2 * Q], F32)
        rs0 = sb("rs0", [P, 2 * Q], F32)
        rs1 = sb("rs1", [P, 2 * Q], F32)
        rs2 = sb("rs2", [P, 2 * Q], F32)
        rstd = sb("rstd", [P, 2 * Q], F32)
        shift = sb("shift", [P, 2 * Q], F32)
        h = sb("h", [P, Q * D], F32)
        hT = sb("hT", [P, Q * N], F32)
        wh = sb("wh", [P, 2, Q * D], F32)
        relu_z = sb("relu_z", [P, Q * N], F32)
        neg_e = sb("neg_e", [P, Q * N], F32)
        neg_max = sb("neg_max", [P, 2, Q], F32)
        prob = sb("prob", [P, Q * N], F32)
        row_sum = sb("row_sum", [P, 2, Q], F32)
        inv_sum = sb("inv_sum", [P, Q], F32)
        probT = sb("probT", [P, Q * N], F32)
        v1m = sb("v1m", [P, Q * D], F32)
        exp_v = sb("exp_v", [P, Q * D], F32)
        pre = sb("pre", [P, Q * D], F32)
        pay = sb("pay", [P, 2, K, Q, ROW], F32)
        h2T = sb("h2T", [P, Q * N], F32)
        logits = sb("logits", [P, Q, E], F32)
        top = sb("top", [P, Q, 8], F32)
        top_i = sb("top_i", [P, Q, 8], U32)
        gap = sb("gap", [P, B], F32)
        chosen = sb("chosen", [P, K, Q, E], F32)
        chosen_h = sb("chosen_h", [P, Q, E], F16)
        group_n = sb("group_n", [P, E], F32)
        count = sb("count", [P, E], F16)
        rank_of = sb("rank_of", [P, K, Q, E], F32)
        pos_f = sb("pos_f", [P, K, Q], F32)
        pos = sb("pos", [P, 2, K, Q], I32)
        gate = sb("gate", [P, K, B], F32)
        exp_gap = sb("exp_gap", [P, B], F32)
        gden = sb("gden", [P, B], F32)
        end_f = sb("end_f", [P, E], F32)
        end_i = sb("end_i", [P, E], I32)
        cnt_i = sb("cnt_i", [P, E], I32)
        ntile_i = sb("ntile_i", [P, E], I32)
        ntile_f = sb("ntile_f", [P, E], F32)
        ones_e = sb("ones_e", [P, E], F32)
        last_tile = sb("last_tile", [P, E], F32)
        skip = sb("skip", [P, E], F32)
        passed = sb("passed", [P, U, E], F32)
        passed_skip = sb("passed_skip", [P, U, E], F32)
        tab = sb("tab", [P, 2, U], F32)
        tab2 = sb("tab2", [P, 2, U], F32)
        tab3 = sb("tab3", [P, 2, U], F32)
        table_e = sb("table_e", [U, P], I32)
        table_r = sb("table_r", [U, P], I32)
        rows = sb("rows", [P, U, ROW], F32)
        xT_hi = sb("xT_hi", [P, 2, P], F32R)
        xT_lo = sb("xT_lo", [P, 2, P], F32R)
        silu = sb("silu", [P, 2, H], F32)
        hid = sb("hid", [P, 2, H], F32)
        hidT = sb("hidT", [P, 2, H], F32)
        y = sb("y", [P, U, D], F32)
        S = 4
        assert S * K * Q * D == E * 2 * D
        res = w3s[:, :].rearrange("p (s k n) -> p s k n", s=S, k=K)

        X_STARTS = [0, 1, 3]
        X_COUNTS = [1, 2, GROUPS - 3]
        x_in = [sem(f"x_in{i}") for i in range(3)]
        gnn_in = sem("gnn_in")
        gate_in = sem("gate_in")
        adj_in = [sem(f"adj_in{i}") for i in range(2)]
        w12_in = [sem(f"w12_in{i}") for i in range(2)]
        w3_in = sem("w3_in")
        scattered = [[sem(f"scattered{i}_{k}") for k in range(K)] for i in range(2)]
        filled = sem("filled")
        rows_in = [sem(f"rows_in{i}") for i in range(U)]
        y_out = [sem(f"y_out{i}") for i in range(U)]
        res_in = [[sem(f"res_in{i}_{k}") for k in range(K)] for i in range(S)]
        out_done = sem("out_done")
        pool_const = sem("pool_const")
        dve_const = sem("dve_const")
        gwT_done = sem("gwT_done")
        gwT_copied = sem("gwT_copied")
        a_spread = sem("a_spread")
        wa_done = sem("wa_done")
        wa_copied = sem("wa_copied")
        w12_hi_done = sem("w12_hi_done")
        w12_lo_done = sem("w12_lo_done")
        mask_done = sem("mask_done")
        stats_done = sem("stats_done")
        rs_done = sem("rs_done")
        h_done = sem("h_done")
        hT_done = sem("hT_done")
        hT_copied = sem("hT_copied")
        z_done = sem("z_done")
        wh_done = sem("wh_done")
        relu_done = sem("relu_done")
        wh_copied = sem("wh_copied")
        e_done = sem("e_done")
        prob_done = sem("prob_done")
        pT_done = sem("pT_done")
        pT_copied = sem("pT_copied")
        o_done = sem("o_done")
        v_done = sem("v_done")
        exp_done = sem("exp_done")
        x2_done = sem("x2_done")
        pay0_done = sem("pay0_done")
        pay1_done = sem("pay1_done")
        h2T_done = sem("h2T_done")
        h2T_copied = sem("h2T_copied")
        logit_done = sem("logit_done")
        chosen_done = sem("chosen_done")
        rank_done = sem("rank_done")
        count_done = sem("count_done")
        pos_done = sem("pos_done")
        ln_done = sem("ln_done")
        rs1_done = sem("rs1_done")
        rs2_done = sem("rs2_done")
        r_done = sem("r_done")
        rstd_done = sem("rstd_done")
        x_stats_done = sem("x_stats_done")
        x2_stats_done = sem("x2_stats_done")
        inv_done = sem("inv_done")
        pre_done = sem("pre_done")
        logit_copied = sem("logit_copied")
        top_done = sem("top_done")
        top_i_done = sem("top_i_done")
        gap_done = sem("gap_done")
        each_chosen = sem("each_chosen")
        group_n_done = sem("group_n_done")
        rank_of_done = sem("rank_of_done")
        pos_f_done = sem("pos_f_done")
        total_done = sem("total_done")
        end_done = sem("end_done")
        tab_step = sem("tab_step")
        tab_done = sem("tab_done")
        gate_step = sem("gate_step")
        tabT_done = sem("tabT_done")
        table_done = sem("table_done")
        gap_exp = sem("gap_exp")
        xT_done = sem("xT_done")
        xT_hi_done = sem("xT_hi_done")
        xT_lo_done = sem("xT_lo_done")
        mlp_done = sem("mlp_done")
        silu_done = sem("silu_done")
        hid_done = sem("hid_done")
        hidT_done = sem("hidT_done")
        hidT_copied = sem("hidT_copied")
        y_done = sem("y_done")
        y_copied = sem("y_copied")
        gated = [sem(f"gated{k}") for k in range(K)]
        first_added = sem("first_added")
        sum_done = sem("sum_done")

        def wait(eng, s, value):
            if not isinstance(value, int) or value > 0:
                eng.wait_ge(s, value)

        def wait_apart(eng, *counts):
            counts = [(s, n if isinstance(n, int) else eng.to_reg(n)) for s, n in counts]
            eng.wait_ge(pool_const, 2)
            for s, n in counts:
                wait(eng, s, n)

        def valid(n, end):
            return not isinstance(n, int) or 0 <= n < end

        def iterations(eng, body):
            for it in range(-2, 4):
                body(it, it % 2)
            with eng.Fori(0, (GROUPS - 6) // 2) as trip:
                body(trip * 2 + 4, 0)
                body(trip * 2 + 5, 1)
            for it in range(GROUPS - 2, GROUPS + 3):
                body(it, it % 2)

        def tiles(eng, body):
            body(-1, U - 2)
            body(-1, U - 1)
            for j in range(U):
                body(0, j)
            with eng.Fori(1, TILES // U - 1) as trip:
                for j in range(U):
                    body(trip, j)
            for j in range(U):
                body(TILES // U - 1, j)
            for j in range(2):
                body(TILES // U, j)

        def tile_at(trip, j, ahead):
            trip, j = trip + (j + ahead) // U, (j + ahead) % U
            return trip * U + j, trip, j

        def slot_sent(g, slot):
            return 8 * Q * (g - slot)

        def cols(t, g, n=Q * D):
            return t[:, bass.ds(g * n, n)]

        def fill_up(eng, first, end):
            ends = [eng.alloc_register(f"end{e}") for e in range(first, end)]
            eng.wait_ge(end_done, 1)
            eng.reg_load(ends, end_i[0:1, first:end])
            for reg in ends:
                row = eng.snap(reg, donate=True, min_val=0, max_val=E * REGION - P)
                eng.dma_start(rows_dram[bass.ds(row, P), :], zero_rows[:, :]).then_inc(filled, 16)

        block = ctx.enter_context(nc.Block())

        @block.sync
        def _(sp):
            x_v = x.rearrange("b n f -> n b f")
            adj_v = adj.rearrange("b n m -> n b m")

            def load_x(g):
                sp.dma_start(x_all[:, g * Q * D:(g + 1) * Q * D].rearrange("p (q f) -> p q f", q=Q),
                             x_v[:, g * Q:(g + 1) * Q, :]).then_inc(x_in[sum(g >= n for n in X_STARTS[1:])], 16)

            def load_weights(e, slot):
                wait(sp, w12_lo_done, e - 1)
                for w, column in ((w1, 0), (w2, H)):
                    sp.dma_start(w12[:, slot, column:column + H],
                                 w[bass.ds(e, 1), :, :].rearrange("e d h -> (e d) h")).then_inc(w12_in[slot], 16)
                sp.dma_start(w3s[:, bass.ds(e * (2 * D), 2 * D)].rearrange("p (c d) -> p c d", c=2),
                             w3[bass.ds(e, 1), :, :].rearrange("e (c p) d -> p (e c) d", c=2)).then_inc(w3_in, 16)

            def load_adj(g, slot):
                wait(sp, mask_done, g - 1)
                sp.dma_start(adj_s[:, slot, :].rearrange("p (q m) -> p q m", q=Q),
                             adj_v[:, bass.ds(g * Q, Q), :]).then_inc(adj_in[slot], 16)

            load_x(0)
            sp.dma_start(gw[:, :], gnn_w).then_inc(gnn_in, 16)
            sp.dma_start(a_col[:, :], gnn_a.rearrange("(k f) o -> f (k o)", k=2),
                         allow_slow_non_contiguous=True).then_inc(gnn_in, 16)
            load_adj(0, 0)
            load_x(1)
            load_adj(1, 1)
            sp.dma_start(gate_ws[:, :], gate_w).then_inc(gate_in, 16)
            for q in range(Q):
                sp.dma_start(bias_row[:, q, :], gate_b.rearrange("(a e) -> a e", a=1)).then_inc(gate_in, 16)
            for g in range(2, GROUPS):
                load_x(g)
            assert E == GROUPS
            load_weights(0, 0)
            with sp.Fori(1, GROUPS // 2) as pair:
                load_adj(pair * 2, 0)
                load_weights(pair * 2 - 1, 1)
                load_adj(pair * 2 + 1, 1)
                load_weights(pair * 2, 0)
            load_weights(E - 1, 1)

            sp.wait_ge(pool_const, 1)
            sp.wait_ge(dve_const, 1)
            sp.dma_start(rows_dram[E * REGION:E * REGION + P, :], zero_rows[:, :]).then_inc(filled, 16)
            fill_up(sp, 0, E // 2)

            def first_row(trip, j):
                return sp.value_load(table_r[j:j + 1, bass.ds(trip, 1)], min_val=0, max_val=E * REGION)

            def load_rows(first, trip, j):
                wait(sp, y_out[j], trip * 16)
                sp.dma_start(rows[:, j, :], rows_dram[bass.ds(first, P), :]).then_inc(rows_in[j], 16)

            AHEAD = 3
            sp.wait_ge(table_done, 1)
            firsts = [first_row(0, j) for j in range(AHEAD)]
            sp.wait_ge(filled, 16 * (E + 1))
            for s in scattered[0] + scattered[1]:
                sp.wait_ge(s, 16 * Q * GROUPS // 2)
            for j in range(U):
                load_rows(firsts[j] if j < AHEAD else first_row(0, j), 0, j)
            with sp.Fori(1, TILES // U) as trip:
                for j in range(U):
                    load_rows(first_row(trip, j), trip, j)

            for s in y_out:
                sp.wait_ge(s, 16 * TILES // U)
            res_v = result_dram.rearrange("(k b n) d -> n k b d", k=K, n=N)

            def load_res(g, s):
                wait(sp, sum_done, g - S + 1)
                for k in range(K):
                    sp.dma_start(res[:, s, k, :].rearrange("p (q d) -> p q d", q=Q),
                                 res_v[:, k, bass.ds(g * Q, Q), :]).then_inc(res_in[s][k], 16)

            for s in range(S):
                load_res(s, s)
            with sp.Fori(1, GROUPS // S) as trip:
                for s in range(S):
                    load_res(trip * S + s, s)
            sp.wait_ge(out_done, 16 * GROUPS)

        @block.gpsimd
        def _(pool):
            nc.gpsimd.memset(ident[:, :], 0.0)
            nc.gpsimd.memset(ones_h[:, :], 1.0)
            nc.gpsimd.memset(before[:, :], 1.0).then_inc(pool_const, 1)
            pool.wait_ge(pool_const, 1)
            nc.gpsimd.affine_select(out=ident[:, :], in_=ident[:, :], compare_op=ALU.not_equal, fill=1.0,
                                    base=0, pattern=[[-1, P]], channel_multiplier=1)
            nc.gpsimd.affine_select(out=before[:, :], in_=before[:, :], compare_op=ALU.is_gt, fill=0.0,
                                    base=0, pattern=[[1, P]], channel_multiplier=-1)
            nc.gpsimd.iota(expert_no[:, :], [[1, E]], base=0, channel_multiplier=0,
                           allow_small_or_imprecise_dtypes=True)
            nc.gpsimd.iota(tile_no[:, :], [[1, U]], base=0, channel_multiplier=U,
                           allow_small_or_imprecise_dtypes=True)
            nc.gpsimd.iota(dest_all[:, :, :], [[TOKENS, K], [N, B]], base=0, channel_multiplier=1)
            nc.gpsimd.iota(count[:, :], [[COUNT_BASE, E]], base=0, channel_multiplier=0,
                           allow_small_or_imprecise_dtypes=True).then_inc(pool_const, 1)

            def scatter(g, slot):
                wait_apart(pool, (pos_done, g + 1),
                           (pay1_done, g + 1))
                for k in range(K):
                    for q in range(Q):
                        nc.gpsimd.indirect_dma_start(
                            out=rows_dram, out_offset=bass.IndirectOffsetOnAxis(
                                ap=pos[:, slot, k, q:q + 1].bitcast(U32), axis=0),
                            in_=pay[:, slot, k, q, :], in_offset=None,
                        ).then_inc(scattered[slot][k], 16)

            with pool.Fori(0, GROUPS // 2) as pair:
                scatter(pair * 2, 0)
                scatter(pair * 2 + 1, 1)

            def send_y(trip, j):
                wait_apart(pool, (y_copied, trip * U + (j + 1)))
                nc.gpsimd.indirect_dma_start(
                    out=result_dram, out_offset=bass.IndirectOffsetOnAxis(
                        ap=rows[:, j, D:D + 1].bitcast(U32), axis=0),
                    in_=y[:, j, :], in_offset=None, bounds_check=NOWHERE - 1, oob_is_err=False,
                ).then_inc(y_out[j], 16)

            with pool.Fori(0, TILES // U) as trip:
                for j in range(U):
                    send_y(trip, j)

            with pool.Fori(0, GROUPS // S) as trip:
                for s in range(S):
                    g = trip * S + s
                    pool.wait_ge(gated[0], g + 1)
                    nc.gpsimd.tensor_tensor(cols(x_all, g), cols(x_all, g), res[:, s, 0, :], ALU.add)\
                        .then_inc(first_added, 1)

        @block.tensor
        def _(pe):
            pe.wait_ge(pool_const, 2)
            pe.wait_ge(gnn_in, 32)
            nc.tensor.transpose(hT_ps[:, 0:P], gw[:, :], ident[:, :]).then_inc(gwT_done, 1)
            pe.wait_ge(gwT_copied, 1)
            pe.wait_ge(a_spread, 1)
            for k in range(2):
                last = nc.tensor.matmul(z_ps[:, k * P:(k + 1) * P], gwT[:, :], a_rep[:, k, :], start=True, stop=True)
            last.then_inc(wa_done, 1)
            pe.wait_ge(wa_copied, 1)

            def body(it, s):
                g = it
                if valid(g, GROUPS):
                    pe.wait_ge(h_done, g + 1)
                    wait(pe, hT_copied, g)
                    for q in range(Q):
                        last = nc.tensor.transpose(hT_ps[:, q * N:(q + 1) * N], h[:, q * D:(q + 1) * D], ident[:, :])
                    last.then_inc(hT_done, 1)
                g = it - 2
                if valid(g, GROUPS):
                    pe.wait_ge(pT_copied, g + 1)
                    pe.wait_ge(wh_copied, g + 1)
                    wait(pe, v_done, g)
                    for q in range(Q):
                        last = nc.tensor.matmul(o_ps[:, q * D:(q + 1) * D], probT[:, q * N:(q + 1) * N],
                                                wh[:, s, q * D:(q + 1) * D], start=True, stop=True)
                    last.then_inc(o_done, 1)
                g = it - 3
                if valid(g, GROUPS):
                    pe.wait_ge(pay0_done, g + 1)
                    wait(pe, h2T_copied, g)
                    for q in range(Q):
                        last = nc.tensor.transpose(h2T_ps[:, q * N:(q + 1) * N], pay[:, 1 - s, 0, q, 0:D], ident[:, :])
                    last.then_inc(h2T_done, 1)
                g = it
                if valid(g, GROUPS):
                    pe.wait_ge(hT_copied, g + 1)
                    wait(pe, e_done, g)
                    nc.tensor.matmul(z_ps[:, :], wa_rep[:, 1, :], hT[:, :], start=True, stop=False,
                                     skip_group_check=True)
                g = it - 1
                if valid(g, GROUPS):
                    pe.wait_ge(prob_done, g + 1)
                    wait(pe, pT_copied, g)
                    for q in range(Q):
                        last = nc.tensor.transpose(pT_ps[:, q * N:(q + 1) * N], prob[:, q * N:(q + 1) * N], ident[:, :])
                    last.then_inc(pT_done, 1)
                g = it
                if valid(g, GROUPS):
                    pe.wait_ge(mask_done, g + 1)
                    for q in range(Q):
                        nc.tensor.matmul(z_ps[:, q * N:(q + 1) * N], hT[:, q * N:(q + 1) * N], wa_rep[:, 0, :],
                                         start=False, stop=False, skip_group_check=True)
                    nc.tensor.matmul(z_ps[:, :], ident_b[:, :], mask[:, s, :], start=False, stop=True,
                                     skip_group_check=True).then_inc(z_done, 1)
                g = it - 3
                if valid(g, GROUPS):
                    if isinstance(g, int) and g == 0:
                        pe.wait_ge(gate_in, 16 * (1 + Q))
                    pe.wait_ge(h2T_copied, g + 1)
                    wait(pe, logit_copied, g)
                    nc.tensor.matmul(logit_ps[:, 0:Q * E], ones_row[:, :], bias_row[:, :, :], start=True, stop=False,
                                     skip_group_check=True)
                    for q in range(Q):
                        last = nc.tensor.matmul(logit_ps[:, q * E:(q + 1) * E], h2T[:, q * N:(q + 1) * N],
                                                gate_ws[:, :], start=False, stop=(q == Q - 1), skip_group_check=True)
                    last.then_inc(logit_done, 1)
                g = it
                if valid(g, GROUPS):
                    wait(pe, wh_copied, g)
                    for q in range(Q):
                        last = nc.tensor.matmul(wh_ps[:, q * D:(q + 1) * D], hT[:, q * N:(q + 1) * N], gw[:, :],
                                                start=True, stop=True)
                    last.then_inc(wh_done, 1)
                g = it - 3
                if valid(g, GROUPS):
                    pe.wait_ge(chosen_done, g + 1)
                    wait(pe, count_done, g)
                    wait(pe, rank_of_done, g)
                    nc.tensor.matmul(rank_ps[:, 0:Q * E], before[:, :], chosen_h[:, :, :], start=True, stop=False,
                                     skip_group_check=True)
                    nc.tensor.matmul(rank_ps[:, 0:Q * E], ones_h[:, :], count[:, :].unsqueeze(1).to_broadcast([P, Q, E]),
                                     start=False, stop=False, skip_group_check=True)
                    for r in range(1, Q):
                        last = nc.tensor.matmul(rank_ps[:, r * E:Q * E], ones_h[:, :], chosen_h[:, 0:Q - r, :],
                                                start=False, stop=(r == Q - 1), skip_group_check=True)
                    last.then_inc(rank_done, 1)

            iterations(pe, body)

            pe.wait_ge(count_done, GROUPS)
            pe.wait_ge(pos_done, GROUPS)
            nc.tensor.matmul(rank_ps[:, 0:E], ones_h[:, :], count[:, :], start=True, stop=True).then_inc(total_done, 1)
            pe.wait_ge(tab_done, 1)
            for k in range(2):
                last = nc.tensor.transpose(logit_ps[0:U, k * P:(k + 1) * P], tab3[:, k, :], ident[:, :])
            last.then_inc(tabT_done, 1)

            pe.wait_ge(table_done, 1)
            pe.wait_ge(w12_lo_done, E)
            pe.wait_ge(w3_in, 16 * E)

            expert_reg = [pe.alloc_register(f"expert{j}") for j in range(U)]
            expert = {}

            def load_expert(trip, j):
                pe.reg_load(expert_reg[j], table_e[j:j + 1, bass.ds(trip, 1)])

            def read_expert(j):
                expert[j] = pe.snap(expert_reg[j], min_val=0, max_val=E - 1)

            load_expert(0, 0)

            def tile(trip, j):
                n, tr, m = tile_at(trip, j, 2)
                if valid(n, TILES):
                    pe.wait_ge(rows_in[m], tr * 16 + 16)
                    nc.tensor.transpose(xT_ps[m % 2][:, 0:P], rows[:, m, 0:D], ident[:, :]).then_inc(xT_done, 1)
                n, tr, m = tile_at(trip, j, -2)
                if valid(n, TILES):
                    if j < 3:
                        read_expert(m)
                    w = w3s[:, bass.ds(expert[m] * (2 * D), 2 * D)]
                    pe.wait_ge(hidT_copied, n + 1)
                    wait(pe, y_copied, n - 1)
                    for c in range(2):
                        last = nc.tensor.matmul(y_ps[m % 2][:, 0:D], hidT[:, m % 2, c * P:(c + 1) * P],
                                                w[:, c * D:(c + 1) * D], start=(c == 0), stop=(c == 1))
                    last.then_inc(y_done, 1)
                n, tr, m = tile_at(trip, j, -1)
                if valid(n, TILES):
                    pe.wait_ge(hid_done, n + 1)
                    for c in range(2):
                        last = nc.tensor.transpose(gT_ps[m % 2][:, c * P:(c + 1) * P],
                                                   hid[:, m % 2, c * P:(c + 1) * P], ident[:, :])
                    last.then_inc(hidT_done, 1)
                n, tr, m = tile_at(trip, j, 1)
                if valid(n, TILES):
                    read_expert(m)
                    w = w12_split[:, bass.ds(expert[m] * W, W)]
                    pe.wait_ge(xT_lo_done, n + 1)
                    for k, (rows_part, w_part) in enumerate(((xT_hi, 0), (xT_lo, 0), (xT_hi, 2 * H))):
                        last = nc.tensor.matmul(mlp_ps[m % 2][:, :], rows_part[:, m % 2, :], w[:, w_part:w_part + 2 * H],
                                                start=(k == 0), stop=(k == 2))
                    last.then_inc(mlp_done, 1)
                n, tr, m = tile_at(trip, j, 2)
                if valid(n, TILES) and not (isinstance(n, int) and n == 0):
                    load_expert(tr, m)

            tiles(pe, tile)

        @block.scalar
        def _(act):
            nc.scalar.preload_act_table_set("natural_log_exp_and_others")
            act.wait_ge(gwT_done, 1)
            nc.scalar.activation(gwT[:, :], hT_ps[:, 0:P], ACT.Copy).then_inc(gwT_copied, 1)
            act.wait_ge(wa_done, 1)
            nc.scalar.activation(wa_rep[:, :, :], z_ps[:, 0:2 * P], ACT.Copy).then_inc(wa_copied, 1)

            def body(it, s):
                g = it
                if valid(g, GROUPS):
                    act.wait_ge(hT_done, g + 1)
                    wait(act, wh_done, g)
                    nc.scalar.activation(hT[:, :], hT_ps[:, :], ACT.Copy).then_inc(hT_copied, 1)
                g = it - 1
                if valid(g, GROUPS):
                    act.wait_ge(e_done, g + 1)
                    wait(act, pT_done, g)
                    for q in range(Q):
                        last = nc.scalar.activation(prob[:, q * N:(q + 1) * N], neg_e[:, q * N:(q + 1) * N], ACT.Exp,
                                                    bias=neg_max[:, 1 - s, q:q + 1], scale=-1.0,
                                                    accum_out=row_sum[:, 1 - s, q:q + 1])
                    last.then_inc(prob_done, 1)
                g = it - 2
                if valid(g, GROUPS):
                    act.wait_ge(v_done, g + 1)
                    wait(act, x2_done, g)
                    nc.scalar.activation(exp_v[:, :], v1m[:, :], ACT.Exp, bias=ones_e[:, 0:1]).then_inc(exp_done, 1)
                g = it - 3
                if valid(g, GROUPS):
                    act.wait_ge(h2T_done, g + 1)
                    wait(act, logit_done, g)
                    nc.scalar.activation(h2T[:, :], h2T_ps[:, :], ACT.Copy).then_inc(h2T_copied, 1)
                g = it + 1
                if valid(g, GROUPS):
                    wait_apart(act, (rstd_done, g + 1),
                               (hT_done, g))
                    for q in range(Q):
                        last = nc.scalar.activation(h[:, q * D:(q + 1) * D], x_all[:, bass.ds(g * (Q * D) + q * D, D)],
                                                    ACT.Identity, bias=shift[:, Q + q:Q + q + 1],
                                                    scale=rstd[:, Q + q:Q + q + 1])
                    last.then_inc(h_done, 1)
                g = it - 1
                if valid(g, GROUPS):
                    act.wait_ge(pT_done, g + 1)
                    wait(act, o_done, g)
                    nc.scalar.activation(probT[:, :], pT_ps[:, :], ACT.Copy).then_inc(pT_copied, 1)
                g = it
                if valid(g, GROUPS):
                    act.wait_ge(z_done, g + 1)
                    wait(act, e_done, g)
                    nc.scalar.activation(relu_z[:, :], z_ps[:, :], ACT.Relu, scale=1 / ALPHA - 1).then_inc(relu_done, 1)
                if valid(it + 2, GROUPS) or valid(it - 2, GROUPS):
                    act.wait_ge(stats_done, it + 3)
                    nc.scalar.activation(lnv[:, :], mv[:, :, 1], ACT.Ln, bias=eps_col[:, 0:1]).then_inc(ln_done, 1)
                    act.wait_ge(ln_done, it + 3)
                    nc.scalar.activation(rs0[:, :], lnv[:, :], ACT.Exp, scale=-0.5).then_inc(rs_done, 1)
                e = it - 1
                if valid(e, E):
                    wait_apart(act, (w12_in[1 - s], (e - (1 - s)) * 16 + 32))
                    nc.scalar.activation(w12_split[:, bass.ds(e * W, 2 * H)], w12[:, 1 - s, :], ACT.Copy).then_inc(w12_hi_done, 1)
                g = it
                if valid(g, GROUPS):
                    act.wait_ge(wh_done, g + 1)
                    wait(act, o_done, g - 1)
                    nc.scalar.activation(wh[:, s, :], wh_ps[:, :], ACT.Copy, bias=-1.0).then_inc(wh_copied, 1)
                g = it - 2
                if valid(g, GROUPS):
                    counts = [(rstd_done, g + 5)]
                    if not isinstance(g, int) or g >= 2:
                        counts += [(scattered[s][0], slot_sent(g, s))]
                    wait_apart(act, *counts)
                    for q in range(Q):
                        last = nc.scalar.activation(pay[:, s, 0, q, 0:D], x_all[:, bass.ds(g * (Q * D) + q * D, D)],
                                                    ACT.Identity, bias=shift[:, q:q + 1], scale=rstd[:, q:q + 1])
                    last.then_inc(pay0_done, 1)

            iterations(act, body)
            act.wait_ge(gap_done, GROUPS)
            nc.scalar.activation(exp_gap[:, :], gap[:, :], ACT.Exp).then_inc(gap_exp, 1)
            fill_up(act, E // 2, E)
            nc.scalar.preload_act_table_set("silu_and_others")

            def tile(trip, j):
                n, tr, m = tile_at(trip, j, 0)
                if valid(n, TILES):
                    act.wait_ge(mlp_done, n + 1)
                    wait(act, hid_done, n - 1)
                    nc.scalar.activation(silu[:, m % 2, :], mlp_ps[m % 2][:, 0:H], ACT.Silu).then_inc(silu_done, 1)
                n, tr, m = tile_at(trip, j, 2)
                if valid(n, TILES):
                    act.wait_ge(xT_done, n + 1)
                    wait(act, mlp_done, n - 1)
                    nc.scalar.activation(xT_hi[:, m % 2, :], xT_ps[m % 2][:, 0:P], ACT.Copy).then_inc(xT_hi_done, 1)
                n, tr, m = tile_at(trip, j, -2)
                if valid(n, TILES):
                    act.wait_ge(y_done, n + 1)
                    wait(act, y_out[m], tr * 16)
                    nc.scalar.activation(y[:, m, :], y_ps[m % 2][:, 0:D], ACT.Copy).then_inc(y_copied, 1)

            tiles(act, tile)

            out_v = out.rearrange("b n f -> n b f")
            with act.Fori(0, GROUPS) as g:
                act.wait_ge(sum_done, g + 1)
                act.dma_start(out_v[:, bass.ds(g * Q, Q), :],
                              cols(x_all, g).rearrange("p (q f) -> p q f", q=Q)).then_inc(out_done, 16)

        @block.vector
        def _(dve):
            nc.vector.memset(eps_col[:, :], EPS)
            nc.vector.memset(ones_row[:, :], 1.0)
            nc.vector.memset(ones_e[:, :], 1.0)
            nc.vector.memset(mv[:, :, :], 1.0)
            nc.vector.memset(pay[:, :, :, :, D + 1:ROW], 0.0)
            nc.vector.memset(zero_rows[:, 0:D], 0.0)
            nc.vector.memset(zero_rows[:, D:ROW].bitcast(I32), NOWHERE).then_inc(dve_const, 1)
            dve.wait_ge(pool_const, 2)
            nc.vector.tensor_copy(ident_b[:, :], ident[:, :])
            nc.vector.tensor_scalar(region_no[:, :], expert_no[:, :], float(REGION), None, ALU.mult)
            dve.wait_ge(gnn_in, 32)
            for k in range(2):
                last = nc.vector.tensor_copy(a_rep[:, k, :], a_col[:, k:k + 1].to_broadcast([P, P]))
            last.then_inc(a_spread, 1)

            def body(it, s):
                newton = valid(it + 2, GROUPS) or valid(it - 2, GROUPS)
                g = it - 2
                if valid(g, GROUPS):
                    xg = cols(x_all, g)
                    dve.wait_ge(prob_done, g + 1)
                    nc.vector.reciprocal(inv_sum[:, :], row_sum[:, s, :]).then_inc(inv_done, 1)
                    dve.wait_ge(o_done, g + 1)
                    dve.wait_ge(inv_done, g + 1)
                    wait(dve, exp_done, g)
                    nc.vector.tensor_tensor(v1m[:, :].rearrange("p (q d) -> p q d", q=Q),
                                            o_ps[:, :].rearrange("p (q d) -> p q d", q=Q),
                                            inv_sum[:, :].unsqueeze(2).to_broadcast([P, Q, D]),
                                            ALU.mult).then_inc(v_done, 1)
                m = it + 1
                if valid(m, GROUPS):
                    dve.wait_ge(adj_in[1 - s], (m - (1 - s)) * 8 + 16)
                    wait(dve, z_done, m - 1)
                    nc.vector.tensor_scalar(mask[:, 1 - s, :], adj_s[:, 1 - s, :], 0, NEG_BIG, ALU.is_le, ALU.mult)\
                        .then_inc(mask_done, 1)
                if valid(g, GROUPS):
                    dve.wait_ge(v_done, g + 1)
                    nc.vector.scalar_tensor_tensor(pre[:, :], v1m[:, :], -1.0, xg, ALU.max, ALU.add).then_inc(pre_done, 1)
                g = it - 3
                if valid(g, GROUPS):
                    counts = [(pay0_done, g + 1)]
                    if not isinstance(g, int) or g >= 2:
                        counts += [(scattered[1 - s][1], slot_sent(g, 1 - s))]
                    wait_apart(dve, *counts)
                    nc.vector.tensor_copy(pay[:, 1 - s, 1, :, 0:D], pay[:, 1 - s, 0, :, 0:D])
                    nc.vector.tensor_copy(pay[:, 1 - s, :, :, D].bitcast(I32), dest_all[:, :, bass.ds(g * Q, Q)])\
                        .then_inc(pay1_done, 1)
                g = it - 2
                if valid(g, GROUPS):
                    dve.wait_ge(exp_done, g + 1)
                    dve.wait_ge(pre_done, g + 1)
                    nc.vector.scalar_tensor_tensor(xg, exp_v[:, :], 1.0, pre[:, :], ALU.min, ALU.add)\
                        .then_inc(x2_done, 1)
                n = it + 2
                if valid(n, GROUPS):
                    for part, start in enumerate(X_STARTS):
                        if isinstance(n, int) and n == start:
                            dve.wait_ge(x_in[part], 16 * X_COUNTS[part])
                    wait_apart(dve, (stats_done, n))
                    for q in range(Q):
                        last = nc.vector.bn_stats(x_stats[:, q, :], x_all[:, bass.ds(n * (Q * D) + q * D, D)])
                    last.then_inc(x_stats_done, 1)
                if valid(g, GROUPS):
                    wait_apart(dve, (x2_done, g + 1))
                    for q in range(Q):
                        last = nc.vector.bn_stats(x2_stats[:, q, :], x_all[:, bass.ds(g * (Q * D) + q * D, D)])
                    last.then_inc(x2_stats_done, 1)
                if valid(n, GROUPS):
                    wait_apart(dve, (x_stats_done, n + 1),
                               (rstd_done, n))
                    for q in range(Q):
                        last = nc.vector.bn_aggr(mv[:, Q + q, :], x_stats[:, q, :])
                    if not valid(g, GROUPS):
                        last.then_inc(stats_done, 1)
                if valid(g, GROUPS):
                    wait_apart(dve, (x2_stats_done, g + 1),
                               (rstd_done, it + 2))
                    for q in range(Q):
                        last = nc.vector.bn_aggr(mv[:, q, :], x2_stats[:, q, :])
                    last.then_inc(stats_done, 1)
                g = it - 3
                if valid(g, GROUPS):
                    dve.wait_ge(logit_done, g + 1)
                    nc.vector.tensor_copy(logits[:, :, :], logit_ps[:, 0:Q * E]).then_inc(logit_copied, 1)
                    wait_apart(dve, (logit_copied, g + 1))
                    for q in range(Q):
                        last = nc.vector.max(top[:, q, :], logits[:, q, :])
                    last.then_inc(top_done, 1)
                    wait_apart(dve, (top_done, g + 1))
                    for q in range(Q):
                        last = nc.vector.max_index(top_i[:, q, :], top[:, q, :], logits[:, q, :])
                    last.then_inc(top_i_done, 1)
                if newton:
                    dve.wait_ge(rs_done, it + 3)
                    nc.vector.scalar_tensor_tensor(rs1[:, :], mv[:, :, 1], EPS, rs0[:, :], ALU.add, ALU.mult)\
                        .then_inc(rs1_done, 1)
                if valid(g, GROUPS):
                    dve.wait_ge(top_i_done, g + 1)
                    nc.vector.tensor_tensor(
                        chosen[:, :, :, :],
                        expert_no[:, :].unsqueeze(1).unsqueeze(1).to_broadcast([P, K, Q, E]),
                        top_i[:, :, 0:K].rearrange("p q k -> p k q").unsqueeze(3).to_broadcast([P, K, Q, E]),
                        ALU.is_equal).then_inc(each_chosen, 1)
                if newton:
                    dve.wait_ge(rs1_done, it + 3)
                    nc.vector.scalar_tensor_tensor(rs2[:, :], rs1[:, :], -0.5, rs0[:, :], ALU.mult, ALU.mult)\
                        .then_inc(rs2_done, 1)
                if valid(g, GROUPS):
                    nc.vector.tensor_tensor(gap[:, bass.ds(g * Q, Q)], top[:, :, 1], top[:, :, 0], ALU.subtract)\
                        .then_inc(gap_done, 1)
                if newton:
                    dve.wait_ge(rs2_done, it + 3)
                    wait(dve, pay0_done, it - 2)
                    if valid(it + 1, GROUPS):
                        wait(dve, h_done, it + 2)
                    nc.vector.scalar_tensor_tensor(rstd[:, :], rs2[:, :], 1.5, rs0[:, :], ALU.add, ALU.mult)\
                        .then_inc(r_done, 1)
                if valid(g, GROUPS):
                    dve.wait_ge(each_chosen, g + 1)
                    wait(dve, rank_done, g)
                    nc.vector.tensor_tensor(chosen_h[:, :, :], chosen[:, 0, :, :], chosen[:, 1, :, :], ALU.add)\
                        .then_inc(chosen_done, 1)
                if newton:
                    dve.wait_ge(r_done, it + 3)
                    nc.vector.scalar_tensor_tensor(shift[:, :], mv[:, :, 0], -1.0, rstd[:, :], ALU.mult, ALU.mult)\
                        .then_inc(rstd_done, 1)
                if valid(g, GROUPS):
                    dve.wait_ge(chosen_done, g + 1)
                    nc.vector.tensor_reduce(group_n[:, :], chosen_h[:, :, :].rearrange("p q e -> p e q"),
                                            AX_X, ALU.add).then_inc(group_n_done, 1)
                g = it
                if valid(g, GROUPS):
                    wait_apart(dve, (relu_done, g + 1),
                               (prob_done, g))
                    for q in range(Q):
                        last = nc.vector.tensor_tensor_reduce(
                            neg_e[:, q * N:(q + 1) * N], z_ps[:, q * N:(q + 1) * N], relu_z[:, q * N:(q + 1) * N],
                            -ALPHA, 3.0e38, ALU.add, ALU.min, neg_max[:, s, q:q + 1])
                    last.then_inc(e_done, 1)
                e = it - 1
                if valid(e, E):
                    wait_apart(dve, (w12_hi_done, e + 1))
                    nc.vector.tensor_tensor(w12_split[:, bass.ds(e * W + 2 * H, 2 * H)], w12[:, 1 - s, :],
                                            w12_split[:, bass.ds(e * W, 2 * H)].bitcast(F32),
                                            ALU.subtract).then_inc(w12_lo_done, 1)
                g = it - 3
                if valid(g, GROUPS):
                    dve.wait_ge(rank_done, g + 1)
                    nc.vector.tensor_tensor(
                        rank_of[:, :, :, :],
                        rank_ps[:, 0:Q * E].rearrange("p (q e) -> p q e", q=Q).unsqueeze(1).to_broadcast([P, K, Q, E]),
                        chosen[:, :, :, :], ALU.mult).then_inc(rank_of_done, 1)
                    dve.wait_ge(group_n_done, g + 1)
                    nc.vector.tensor_tensor(count[:, :], count[:, :], group_n[:, :], ALU.add).then_inc(count_done, 1)
                    dve.wait_ge(rank_of_done, g + 1)
                    nc.vector.tensor_reduce(pos_f[:, :, :], rank_of[:, :, :, :], AX_X, ALU.add).then_inc(pos_f_done, 1)
                    dve.wait_ge(pos_f_done, g + 1)
                    nc.vector.tensor_copy(pos[:, 1 - s, :, :], pos_f[:, :, :]).then_inc(pos_done, 1)

            iterations(dve, body)

            dve.wait_ge(total_done, 1)
            nc.vector.tensor_copy(end_i[:, :], rank_ps[:, 0:E]).then_inc(end_done, 1)
            nc.vector.scalar_tensor_tensor(cnt_i[:, :], rank_ps[:, 0:E], float(P - 1), region_no[:, :],
                                           ALU.add, ALU.subtract).then_inc(tab_step, 1)
            dve.wait_ge(tab_step, 1)
            nc.vector.tensor_scalar(ntile_i[:, :], cnt_i[:, :], 7, None, ALU.arith_shift_right).then_inc(tab_step, 1)
            dve.wait_ge(tab_step, 2)
            nc.vector.tensor_copy(ntile_f[:, :], ntile_i[:, :]).then_inc(tab_step, 1)
            dve.wait_ge(tab_step, 3)
            nc.vector.tensor_tensor_scan(last_tile[:, :], ones_e[:, :], ntile_f[:, :], 0.0, ALU.mult, ALU.add)
            nc.vector.tensor_scalar(skip[:, :], ntile_f[:, :], -float(P), float(REGION), ALU.mult, ALU.add)\
                .then_inc(tab_step, 1)
            dve.wait_ge(tab_step, 4)
            nc.vector.tensor_tensor(passed[:, :, :], tile_no[:, :].unsqueeze(2).to_broadcast([P, U, E]),
                                    last_tile[:, :].unsqueeze(1).to_broadcast([P, U, E]), ALU.is_ge)\
                .then_inc(tab_step, 1)
            dve.wait_ge(tab_step, 5)
            nc.vector.tensor_tensor(passed_skip[:, :, :], passed[:, :, :],
                                    skip[:, :].unsqueeze(1).to_broadcast([P, U, E]), ALU.mult)
            nc.vector.tensor_reduce(tab[:, 0, :], passed[:, :, :], AX_X, ALU.add).then_inc(tab_step, 1)
            dve.wait_ge(tab_step, 6)
            nc.vector.tensor_reduce(tab[:, 1, :], passed_skip[:, :, :], AX_X, ALU.add)
            nc.vector.tensor_scalar(tab3[:, 0, :], tab[:, 0, :], float(E - 1), None, ALU.min).then_inc(tab_step, 1)
            dve.wait_ge(tab_step, 7)
            nc.vector.scalar_tensor_tensor(tab2[:, 1, :], tile_no[:, :], float(P), tab[:, 1, :], ALU.mult, ALU.add)\
                .then_inc(tab_step, 1)
            dve.wait_ge(tab_step, 8)
            nc.vector.tensor_scalar(tab3[:, 1, :], tab2[:, 1, :], float(E * REGION), None, ALU.min).then_inc(tab_done, 1)
            dve.wait_ge(tabT_done, 1)
            nc.vector.tensor_copy(table_e[:, :], logit_ps[0:U, 0:P])
            nc.vector.tensor_copy(table_r[:, :], logit_ps[0:U, P:2 * P]).then_inc(table_done, 1)

            dve.wait_ge(gap_exp, 1)
            nc.vector.tensor_scalar(gden[:, :], exp_gap[:, :], 1.0, None, ALU.add).then_inc(gate_step, 1)
            dve.wait_ge(gate_step, 1)
            nc.vector.reciprocal(gate[:, 0, :], gden[:, :]).then_inc(gate_step, 1)
            dve.wait_ge(gate_step, 2)
            nc.vector.tensor_tensor(gate[:, 1, :], exp_gap[:, :], gate[:, 0, :], ALU.mult).then_inc(gate_step, 1)

            def tile(trip, j):
                n, tr, m = tile_at(trip, j, 0)
                if valid(n, TILES):
                    dve.wait_ge(silu_done, n + 1)
                    wait(dve, hidT_done, n - 1)
                    nc.vector.tensor_tensor(hid[:, m % 2, :], silu[:, m % 2, :], mlp_ps[m % 2][:, H:2 * H], ALU.mult)\
                        .then_inc(hid_done, 1)
                n, tr, m = tile_at(trip, j, -1)
                if valid(n, TILES):
                    dve.wait_ge(hidT_done, n + 1)
                    wait(dve, y_done, n - 1)
                    nc.vector.tensor_copy(hidT[:, m % 2, :], gT_ps[m % 2][:, 0:H]).then_inc(hidT_copied, 1)
                n, tr, m = tile_at(trip, j, 2)
                if valid(n, TILES):
                    dve.wait_ge(xT_hi_done, n + 1)
                    nc.vector.tensor_tensor(xT_lo[:, m % 2, :], xT_ps[m % 2][:, 0:P], xT_hi[:, m % 2, :].bitcast(F32),
                                            ALU.subtract).then_inc(xT_lo_done, 1)

            tiles(dve, tile)

            dve.wait_ge(gate_step, 3)

            def gate_result(trip, s, k):
                dve.wait_ge(res_in[s][k], trip * 16 + 16)
                r = res[:, s, k, :].rearrange("p (q d) -> p q d", q=Q)
                nc.vector.tensor_tensor(r, r, gate[:, k, bass.ds((trip * S + s) * Q, Q)].unsqueeze(2).to_broadcast([P, Q, D]),
                                        ALU.mult).then_inc(gated[k], 1)

            def add_second(g, s):
                dve.wait_ge(first_added, g + 1)
                dve.wait_ge(gated[1], g + 1)
                nc.vector.tensor_tensor(cols(x_all, g), cols(x_all, g), res[:, s, 1, :], ALU.add).then_inc(sum_done, 1)

            for s in range(S):
                gate_result(0, s, 0)
                if s > 0:
                    add_second(s - 1, s - 1)
                gate_result(0, s, 1)
            with dve.Fori(1, GROUPS // S) as trip:
                for s in range(S):
                    gate_result(trip, s, 0)
                    add_second(trip * S + (s - 1), (s - 1) % S)
                    gate_result(trip, s, 1)
            add_second(GROUPS - 1, S - 1)


_INS = ["x", "adj", "L0_gnn_W", "L0_gnn_a", "L0_ffn_gate_w", "L0_ffn_gate_b", "L0_ffn_w1", "L0_ffn_w2", "L0_ffn_w3"]


def kernel(**inputs):
    import numpy as np
    import concourse.bacc as bacc
    from concourse.bass_utils import run_bass_kernel_spmd

    nc = bacc.Bacc("TRN2", target_bir_lowering=False, num_devices=1)
    arrays, args = {}, []
    for name in _INS:
        a = np.ascontiguousarray(inputs[name])
        arrays[f"in_{name}"] = a
        args.append(nc.dram_tensor(f"in_{name}", a.shape, mybir.dt.from_np(a.dtype), kind="ExternalInput").ap())
    x = arrays["in_x"]
    args.append(nc.dram_tensor("out", x.shape, mybir.dt.from_np(x.dtype), kind="ExternalOutput").ap())
    gnn_moe_kernel(nc, *args)
    r = run_bass_kernel_spmd(nc, [arrays], core_ids=[0])
    return r.results[0]["out"]
```
